# Optimizing a Trainium2 kernel written in Bass

```python
import numpy as np
import jax
import jax.numpy as jnp

def _softmax(x, axis=-1):
    return jax.nn.softmax(x, axis=axis)

def _gelu(x):
    return jax.nn.gelu(x, approximate=True)

def _silu(x):
    return jax.nn.silu(x)

def _sigmoid(x):
    return jax.nn.sigmoid(x)

def _layernorm(x, axis=-1, eps=1e-05):
    m = jnp.mean(x, axis=axis, keepdims=True)
    v = jnp.var(x, axis=axis, keepdims=True)
    return (x - m) / jnp.sqrt(v + eps)

def _scatter_add(tgt, idx, src, axis=0):
    return tgt.at[idx].add(src)

def _segment_sum(src, seg, n):
    return jax.ops.segment_sum(src, seg, n)
kernel_name = 'mk_seq_postln_d1_jaxref_r8_cc7ee3'

def setup_inputs(seed: int=0):
    np.random.seed(seed)
    _w = jnp.asarray

    def _L0_attn_setup():
        import jax, jax.numpy as jnp
        import numpy as np
        EMBED_DIM = 128
        NUM_HEADS = 16
        HEAD_DIM = EMBED_DIM // NUM_HEADS
        WL_CHANNELS = 16
        BATCH = 1
        SEQ = 128
        KERR = 2.7e-18 * 1000000.0
        SCALE = 1.0 / np.sqrt(HEAD_DIM)
        W_INIT = 0.02
        key = jax.random.key(seed)
        ks = jax.random.split(key, 7)
        x = jax.random.normal(ks[0], (BATCH, SEQ, EMBED_DIM), dtype=jnp.float32)
        Wq = jax.random.normal(ks[1], (EMBED_DIM, EMBED_DIM), dtype=jnp.float32) * W_INIT
        Wk = jax.random.normal(ks[2], (EMBED_DIM, EMBED_DIM), dtype=jnp.float32) * W_INIT
        Wv = jax.random.normal(ks[3], (EMBED_DIM, EMBED_DIM), dtype=jnp.float32) * W_INIT
        Wo = jax.random.normal(ks[4], (EMBED_DIM, EMBED_DIM), dtype=jnp.float32) * W_INIT
        bq = jnp.zeros((EMBED_DIM,), jnp.float32)
        bk = jnp.zeros((EMBED_DIM,), jnp.float32)
        bv = jnp.zeros((EMBED_DIM,), jnp.float32)
        bo = jnp.zeros((EMBED_DIM,), jnp.float32)
        phase_modulators = jax.random.normal(ks[5], (WL_CHANNELS, NUM_HEADS), dtype=jnp.float32)
        interference_weights = jnp.ones((WL_CHANNELS,), jnp.float32)
        return {'x': x, 'Wq': Wq, 'bq': bq, 'Wk': Wk, 'bk': bk, 'Wv': Wv, 'bv': bv, 'Wo': Wo, 'bo': bo, 'phase_modulators': phase_modulators, 'interference_weights': interference_weights}
    _L0_attn_in = _L0_attn_setup()

    def _L0_ffn_setup():
        import jax, jax.numpy as jnp
        import numpy as np
        TOP_K = 2
        key = jax.random.key(seed)
        ks = jax.random.split(key, 5)
        B, T, D, F, E = (2, 256, 128, 512, 8)
        x = jax.random.normal(ks[0], (B, T, D), dtype=jnp.float32)
        router_w = jax.random.normal(ks[1], (D, E + 1), dtype=jnp.float32) * 0.02
        router_b = jax.random.normal(ks[2], (E + 1,), dtype=jnp.float32) * 0.02
        w1 = jax.random.normal(ks[3], (E, D, F), dtype=jnp.float32) * 0.02
        w2 = jax.random.normal(ks[4], (E, F, D), dtype=jnp.float32) * 0.02
        return {'x': x, 'router_w': router_w, 'router_b': router_b, 'w1': w1, 'w2': w2}
    _L0_ffn_in = _L0_ffn_setup()
    _d = {'L0_attn_x': _L0_attn_in['x'], 'L0_attn_Wq': _L0_attn_in['Wq'], 'L0_attn_bq': _L0_attn_in['bq'], 'L0_attn_Wk': _L0_attn_in['Wk'], 'L0_attn_bk': _L0_attn_in['bk'], 'L0_attn_Wv': _L0_attn_in['Wv'], 'L0_attn_bv': _L0_attn_in['bv'], 'L0_attn_Wo': _L0_attn_in['Wo'], 'L0_attn_bo': _L0_attn_in['bo'], 'L0_attn_phase_modulators': _L0_attn_in['phase_modulators'], 'L0_attn_interference_weights': _L0_attn_in['interference_weights'], 'L0_ffn_router_w': _L0_ffn_in['router_w'], 'L0_ffn_router_b': _L0_ffn_in['router_b'], 'L0_ffn_w1': _L0_ffn_in['w1'], 'L0_ffn_w2': _L0_ffn_in['w2']}
    _x0 = _d['L0_attn_x']
    _d['L0_attn_x'] = jax.random.normal(jax.random.fold_in(jax.random.key(seed), 1), (4, 1024, 128), dtype=_x0.dtype)
    del _x0
    return _d

def reference(L0_attn_x, L0_attn_Wq, L0_attn_bq, L0_attn_Wk, L0_attn_bk, L0_attn_Wv, L0_attn_bv, L0_attn_Wo, L0_attn_bo, L0_attn_phase_modulators, L0_attn_interference_weights, L0_ffn_router_w, L0_ffn_router_b, L0_ffn_w1, L0_ffn_w2):

    def _L0_attn_ref(x, Wq, bq, Wk, bk, Wv, bv, Wo, bo, phase_modulators, interference_weights):
        import jax, jax.numpy as jnp
        import numpy as np
        EMBED_DIM = 128
        NUM_HEADS = 16
        HEAD_DIM = EMBED_DIM // NUM_HEADS
        WL_CHANNELS = 16
        BATCH = 1
        SEQ = 128
        KERR = 2.7e-18 * 1000000.0
        SCALE = 1.0 / np.sqrt(HEAD_DIM)
        W_INIT = 0.02
        B, S, E = x.shape
        H, D = (NUM_HEADS, HEAD_DIM)

        def proj(W, b):
            y = jnp.einsum('bse,ef->bsf', x, W) + b
            return y.reshape(B, S, H, D).transpose(0, 2, 1, 3)
        Q = proj(Wq, bq)
        K = proj(Wk, bk)
        V = proj(Wv, bv)
        cos_pm = jnp.cos(phase_modulators)

        def wl_step(acc, wl):
            cpm, iw = wl
            m = cpm[None, :, None, None]
            Qw = Q * m
            Kw = K * m
            scores = jnp.einsum('bhqd,bhkd->bhqk', Qw, Kw) * SCALE
            scores = scores * jnp.cos(KERR * scores * scores)
            attn = jax.nn.softmax(scores, axis=-1)
            out = jnp.einsum('bhqk,bhkd->bhqd', attn, V)
            return (acc + out * iw, None)
        acc0 = jnp.zeros((B, H, S, D), x.dtype)
        acc, _ = jax.lax.scan(wl_step, acc0, (cos_pm, interference_weights))
        combined = acc / WL_CHANNELS
        combined = combined.transpose(0, 2, 1, 3).reshape(B, S, E)
        return jnp.einsum('bse,ef->bsf', combined, Wo) + bo

    def _L0_ffn_ref(x, router_w, router_b, w1, w2):
        import jax, jax.numpy as jnp
        import numpy as np
        TOP_K = 2
        E = w1.shape[0]
        logits = x @ router_w + router_b
        probs = jax.nn.softmax(logits, axis=-1)
        top_v, top_i = jax.lax.top_k(probs, TOP_K)
        gates = jnp.sum(jax.nn.one_hot(top_i, E + 1, dtype=x.dtype) * top_v[..., None], axis=-2)
        h = jax.nn.gelu(jnp.einsum('btd,edf->ebtf', x, w1), approximate=False)
        y = jnp.einsum('ebtf,efd->ebtd', h, w2)
        out = jnp.einsum('bte,ebtd->btd', gates[..., :E], y) + gates[..., E:] * x
        return out
    x = L0_attn_x
    x = _layernorm(x + _L0_attn_ref(x, L0_attn_Wq, L0_attn_bq, L0_attn_Wk, L0_attn_bk, L0_attn_Wv, L0_attn_bv, L0_attn_Wo, L0_attn_bo, L0_attn_phase_modulators, L0_attn_interference_weights), axis=-1)
    x = _layernorm(x + _L0_ffn_ref(x, L0_ffn_router_w, L0_ffn_router_b, L0_ffn_w1, L0_ffn_w2), axis=-1)
    return x

_drawn_inputs = setup_inputs


def setup_inputs(seed=0):
    import zlib

    import numpy as np

    out = dict(_drawn_inputs(seed))
    spreads = {'L0_attn_bq': (0.0, 0.8),
     'L0_attn_bk': (0.0, 0.8),
     'L0_attn_bv': (0.0, 0.375),
     'L0_attn_bo': (0.0, 0.1),
     'L0_attn_interference_weights': (1.0, 0.6)}
    factors = {'L0_attn_Wq': 8.0,
     'L0_attn_Wk': 8.0,
     'L0_attn_Wv': 8.0,
     'L0_attn_Wo': 2.925,
     'L0_attn_phase_modulators': 8.0,
     'L0_ffn_router_w': 6.429,
     'L0_ffn_router_b': 8.0,
     'L0_ffn_w1': 5.623,
     'L0_ffn_w2': 5.541}
    for name, (base, spread) in spreads.items():
        noise = np.random.default_rng([zlib.crc32(name.encode()), seed]).standard_normal(out[name].shape)
        drawn = base * np.exp(spread * noise) if base else spread * noise
        out[name] = jnp.asarray(drawn.astype(out[name].dtype))
    for name, factor in factors.items():
        out[name] = (out[name] * factor).astype(out[name].dtype)
    return out
```

```python
from contextlib import ExitStack

import numpy as np
import concourse.bass as bass
from concourse import mybir

FP32 = mybir.dt.float32
I32 = mybir.dt.int32
ALU = mybir.AluOpType
ACT = mybir.ActivationFunctionType
AX = mybir.AxisListType

P = 128
B, S, E = 4, 1024, 128
H, D, W = 16, 8, 16
NE, F, NR = 8, 512, 9
KT = S // P
HALF = 512
NH = B * H
VC = 32
G = 4
QG = S // G
NCH = 2 * W
CK = KT // 2
SLOTS = 4
GT = 4
NG = B * S // (GT * P)
FC = F // P
SCALE = 1.0 / np.sqrt(D)
KERR = 2.7e-18 * 1000000.0
EPS = 1e-5
SAFE_SCORE = 9000.0
SAFE_PRODUCT = SAFE_SCORE / (SCALE * D)
MAGIC = 1.5 * 2.0 ** 23
TWO_PI = (6.28125, 0.0019352436065673828, 6.357301884918343e-08)
PI = 3.1415925
RSQRT_SEED = float(0x5F3759DF)
START = 1
SP_FULLS, SP_FREES = KT + 2, KT + 1


def build(nc, x, wq, bq, wk, bk, wv, bv, wo, bo, pm, iw, rw, rb, w1, w2, out):
    qt_dram = nc.dram_tensor("qt_scratch", (B, P, S), FP32, kind="Internal").ap()
    kt_dram = nc.dram_tensor("kt_scratch", (B, P, S), FP32, kind="Internal").ap()
    v_dram = nc.dram_tensor("v_scratch", (B, P, KT, E), FP32, kind="Internal").ap()
    att_dram = nc.dram_tensor("att_scratch", (B * S // P, P, E), FP32, kind="Internal").ap()
    x_tiles = x.rearrange("b (t p) e -> (b t) p e", p=P)
    out_tiles = out.rearrange("b (t p) e -> (b t) p e", p=P)

    ctx = ExitStack()
    with ctx:
        def sb(name, shape, dt=FP32):
            return ctx.enter_context(nc.sbuf_tensor(name, shape, dt))

        def ps(name, shape):
            return ctx.enter_context(nc.psum_tensor(name, shape, FP32))

        def sem(name):
            return ctx.enter_context(nc.semaphore(name))

        ident = sb("ident", [P, P])
        headmask = sb("headmask", [P, H])
        rank = sb("rank", [P, NR])
        scales = sb("scales", [P, W * H])
        pm_sb = sb("pm_sb", [P, W * H])
        trig = sb("trig", [P, W * H])
        wl_weight = sb("wl_weight", [P, W])
        wq_sb, wk_sb, wv_sb, wo_sb = (sb(n, [P, E]) for n in ("wq_sb", "wk_sb", "wv_sb", "wo_sb"))
        bq_sb, bk_sb = sb("bq_sb", [P, 1]), sb("bk_sb", [P, 1])
        bv_sb, bo_sb = sb("bv_sb", [P, E]), sb("bo_sb", [P, E])
        rw_sb, rb_sb = sb("rw_sb", [P, NR]), sb("rb_sb", [P, NR])
        peak = sb("peak", [P, 2 * B])
        peak_row = sb("peak_row", [1, 2])
        product = sb("product", [1, 1])
        flag = sb("flag", [1, 1], I32)

        qt = sb("qt", [P, S])
        kt_ = sb("kt_", [P, S])
        vv = sb("vv", [P, KT, E])
        km = sb("km", [P, S])
        scores = sb("scores", [P, 2, KT, S])
        ring = sb("ring", [P, SLOTS, CK * S])
        vh = sb("vh", [P, KT, VC])
        colmax = sb("colmax", [P, S])
        rowmax = sb("rowmax", [P, KT])
        numer = sb("numer", [P, 2, HALF])
        recip = sb("recip", [P, 4, 8])
        coef = sb("coef", [P, 4, 8])
        parts = sb("parts", [P, W, 8, D])
        att = sb("att", [P, KT, E])

        pv = ps("pv", [P, 2, HALF])
        tr = ps("tr", [P, 2, HALF])
        sc = ps("sc", [P, 2, S])

        consts_loaded = sem("consts_loaded")
        consts_made = sem("consts_made")
        mask_zeroed = sem("mask_zeroed")
        flag_ready = sem("flag_ready")

        block = ctx.enter_context(nc.Block())

        def apart(engine):
            engine.nop(nofuse=True)

        scale_step = sem("scale_step")
        sine_ready = sem("sine_ready")
        x_loaded = sem("x_loaded")
        xT_ready, xT_made = sem("xT_ready"), sem("xT_made")
        q_mm, k_mm, v_mm = sem("q_mm"), sem("k_mm"), sem("v_mm")
        q_made, k_made, v_made = sem("q_made"), sem("k_made"), sem("v_made")
        peak_made = sem("peak_made")
        qkv_stored = sem("qkv_stored")
        peak_rows, peak_step = sem("peak_rows"), sem("peak_step")
        xa = scores[:, 0, 0, :].rearrange("p (t e) -> p t e", e=E)
        xT = scores[:, 0, 1, :]
        CONST_DMAS = 12

        def sync_setup(sp):
            def everywhere(ap, n):
                return ap.rearrange("(o n) -> o n", o=1).to_broadcast([P, n])
            loads = [(wq_sb[:, :], wq), (wk_sb[:, :], wk), (wv_sb[:, :], wv), (wo_sb[:, :], wo),
                     (bq_sb[:, :], bq.rearrange("(p o) -> p o", o=1)),
                     (bk_sb[:, :], bk.rearrange("(p o) -> p o", o=1)),
                     (bv_sb[:, :], everywhere(bv, E)), (bo_sb[:, :], everywhere(bo, E)),
                     (rw_sb[:, :], rw), (rb_sb[:, :], everywhere(rb, NR)),
                     (pm_sb[:, :], everywhere(pm.rearrange("w h -> (w h)"), W * H)),
                     (wl_weight[:, :], everywhere(iw, W))]
            for dst, src in loads:
                sp.dma_start(dst, src).then_inc(consts_loaded, 16)
            with sp.Fori(0, B) as b:
                sp.wait_ge(xT_ready, b + START)
                sp.dma_start(xa, x_tiles[bass.ds(b * KT, KT)].rearrange("t p e -> p t e")).then_inc(x_loaded, 16)
                sp.wait_ge(q_made, b + 1 + START)
                sp.dma_start(qt_dram[bass.ds(b, 1)].rearrange("o p s -> p (o s)"), qt[:, :]).then_inc(qkv_stored, 16)
                sp.wait_ge(k_made, b + 1 + START)
                sp.dma_start(kt_dram[bass.ds(b, 1)].rearrange("o p s -> p (o s)"), kt_[:, :]).then_inc(qkv_stored, 16)
                sp.wait_ge(v_made, b + 1 + START)
                sp.dma_start(v_dram[bass.ds(b, 1)].rearrange("o p t e -> p (o t) e"), vv[:, :, :]).then_inc(qkv_stored, 16)

        def pool_setup(pool):
            for started in (xT_ready, q_made, k_made, v_mm, v_made, peak_made, qkv_stored, probs_ready, tr_full,
                            tr_read, att_made, att_stored, gen_scores, gen_tr, ff_x1, ff_gelu, ff_expert,
                            ff_added, ff_stored):
                pool.sem_inc(started, START)
            nc.gpsimd.memset(ident[:, :], 1.0)
            nc.gpsimd.memset(headmask[:, :], 1.0)
            for e in range(NR):
                nc.gpsimd.memset(rank[:, e:e + 1], float(NR - e))
            nc.gpsimd.memset(vh[:, :, :], 0.0).then_inc(mask_zeroed, 1)
            pool.wait_ge(mask_zeroed, 1)
            nc.gpsimd.memset(vh[:, :, D:D + 1], 1.0)
            nc.gpsimd.affine_select(out=ident[:, :], in_=ident[:, :], compare_op=ALU.is_equal, fill=0.0,
                                    base=0, pattern=[[-1, P]], channel_multiplier=1)
            nc.gpsimd.affine_select(out=headmask[:, :], in_=headmask[:, :], compare_op=ALU.is_ge, fill=0.0,
                                    base=0, pattern=[[-D, H]], channel_multiplier=1).then_inc(mask_zeroed, 1)
            pool.wait_ge(mask_zeroed, 2)
            nc.gpsimd.affine_select(out=headmask[:, :], in_=headmask[:, :], compare_op=ALU.is_ge, fill=0.0,
                                    base=D - 1, pattern=[[D, H]], channel_multiplier=-1).then_inc(consts_made, 1)

        def scalar_setup(act):
            act.wait_ge(scale_step, 5)
            nc.scalar.activation(trig[:, :], trig[:, :], ACT.Sin, scale=0.5).then_inc(sine_ready, 1)
            act.wait_ge(consts_loaded, 16 * CONST_DMAS)
            act.preload_act_table(ACT.Exp)
            with act.Fori(0, B) as b:
                act.wait_ge(q_mm, b + 1)
                act.wait_ge(qkv_stored, 48 * b + START)
                act.wait_ge(peak_made, b + START)
                nc.scalar.activation(qt[:, :], sc[:, 1, :], ACT.Identity, bias=bq_sb[:, 0:1]).then_inc(q_made, 1)
                act.wait_ge(k_mm, b + 1)
                nc.scalar.activation(kt_[:, :], sc[:, 0, :], ACT.Identity, bias=bk_sb[:, 0:1]).then_inc(k_made, 1)

        def tensor_setup(pe):
            pe.wait_ge(consts_made, 1)
            pe.wait_ge(consts_loaded, 16 * CONST_DMAS)
            with pe.Fori(0, B) as b:
                pe.wait_ge(x_loaded, 16 * (b + 1))
                pe.wait_ge(k_made, b + START)
                for t in range(KT):
                    last = nc.tensor.transpose(sc[:, 0, t * P:(t + 1) * P], xa[:, t, :], ident[:, :])
                last.then_inc(xT_ready, 1)
                pe.wait_ge(xT_made, b + 1)
                pe.wait_ge(q_made, b + START)
                for half in range(2):
                    cols = slice(half * HALF, (half + 1) * HALF)
                    last = nc.tensor.matmul(sc[:, 1, cols], wq_sb[:, :], xT[:, cols], start=True, stop=True)
                last.then_inc(q_mm, 1)
                for half in range(2):
                    cols = slice(half * HALF, (half + 1) * HALF)
                    last = nc.tensor.matmul(sc[:, 0, cols], wk_sb[:, :], xT[:, cols], start=True, stop=True)
                last.then_inc(k_mm, 1)
                pe.wait_ge(v_made, b + START)
                for t in range(KT):
                    last = nc.tensor.matmul(tr[:, t // 4, (t % 4) * P:(t % 4 + 1) * P], xT[:, t * P:(t + 1) * P],
                                            wv_sb[:, :], start=True, stop=True)
                last.then_inc(v_mm, 1)
            pe.wait_ge(peak_step, 1)
            for i in range(2):
                last = nc.tensor.matmul(pv[0:1, 0, i * P:(i + 1) * P], peak[:, i:i + 1], ident[:, :],
                                        start=True, stop=True)
            last.then_inc(peak_rows, 1)

        def vector_setup(dve):
            dve.wait_ge(consts_loaded, 16 * CONST_DMAS)
            whole = colmax[:, 0:W * H]
            nc.vector.tensor_scalar(wl_weight[:, :], wl_weight[:, :], 1.0 / W, None, ALU.mult)
            nc.vector.tensor_scalar(whole, pm_sb[:, :], 1.0 / (2.0 * np.pi), MAGIC, ALU.mult, ALU.add).then_inc(scale_step, 1)
            dve.wait_ge(scale_step, 1)
            nc.vector.tensor_scalar(whole, whole, MAGIC, None, ALU.subtract).then_inc(scale_step, 1)
            src = pm_sb[:, :]
            for i, part in enumerate(TWO_PI):
                dve.wait_ge(scale_step, 2 + i)
                nc.vector.scalar_tensor_tensor(trig[:, :], whole, -part, src, ALU.mult, ALU.add).then_inc(scale_step, 1)
                src = trig[:, :]
            dve.wait_ge(sine_ready, 1)
            nc.vector.tensor_tensor(pm_sb[:, :], trig[:, :], trig[:, :], ALU.mult).then_inc(scale_step, 1)
            dve.wait_ge(scale_step, 6)
            nc.vector.tensor_scalar(trig[:, :], pm_sb[:, :], -2.0, 1.0, ALU.mult, ALU.add).then_inc(scale_step, 1)
            dve.wait_ge(scale_step, 7)
            nc.vector.tensor_tensor(pm_sb[:, :], trig[:, :], trig[:, :], ALU.mult).then_inc(scale_step, 1)
            dve.wait_ge(scale_step, 8)
            nc.vector.tensor_scalar(scales[:, :], pm_sb[:, :], SCALE, None, ALU.mult).then_inc(scale_step, 1)
            with dve.Fori(0, B) as b:
                dve.wait_ge(xT_ready, b + 1 + START)
                dve.wait_ge(v_mm, b + START)
                nc.vector.tensor_copy(xT, sc[:, 0, :]).then_inc(xT_made, 1)
                dve.wait_ge(v_mm, b + 1 + START)
                dve.wait_ge(qkv_stored, 48 * b + START)
                nc.vector.tensor_tensor(vv[:, :, :], tr[:, :, :].rearrange("p a (t e) -> p (a t) e", e=E),
                                        bv_sb[:, :].rearrange("p (o e) -> p o e", o=1).to_broadcast([P, KT, E]),
                                        ALU.add).then_inc(v_made, 1)
                dve.wait_ge(q_made, b + 1 + START)
                nc.vector.tensor_reduce(peak[:, bass.ds(b, 1)], qt[:, :], axis=AX.X, op=ALU.max,
                                        apply_absolute_value=True)
                dve.wait_ge(k_made, b + 1 + START)
                nc.vector.tensor_reduce(peak[:, bass.ds(b + B, 1)], kt_[:, :], axis=AX.X, op=ALU.max,
                                        apply_absolute_value=True).then_inc(peak_made, 1)
            dve.wait_ge(peak_made, B + START)
            nc.vector.tensor_reduce(recip[:, 0, 0:2], peak[:, :].rearrange("p (i b) -> p i b", b=B), axis=AX.X, op=ALU.max).then_inc(peak_made, 1)
            dve.wait_ge(peak_made, B + 1 + START)
            nc.vector.tensor_copy(peak[:, 0:2], recip[:, 0, 0:2]).then_inc(peak_step, 1)
            dve.wait_ge(peak_rows, 1)
            nc.vector.tensor_reduce(peak_row[:, :], pv[0:1, 0, 0:2 * P].rearrange("p (i q) -> p i q", q=P), axis=AX.X,
                                    op=ALU.max).then_inc(peak_step, 1)
            dve.wait_ge(peak_step, 2)
            nc.vector.tensor_tensor(product[:, :], peak_row[:, 0:1], peak_row[:, 1:2], ALU.mult).then_inc(peak_step, 1)
            dve.wait_ge(peak_step, 3)
            nc.vector.tensor_scalar(flag[:, :], product[:, :], SAFE_PRODUCT, None, ALU.is_lt).then_inc(flag_ready, 1)

        qk_loaded, v_loaded = sem("qk_loaded"), sem("v_loaded")
        att_made, att_stored = sem("att_made"), sem("att_stored")

        def load_qk(sp, b):
            sp.dma_start(qt[:, :], qt_dram[bass.ds(b, 1)].rearrange("o p s -> p (o s)")).then_inc(qk_loaded, 16)
            sp.dma_start(kt_[:, :], kt_dram[bass.ds(b, 1)].rearrange("o p s -> p (o s)")).then_inc(qk_loaded, 16)

        def load_v(sp, b):
            sp.dma_start(vv[:, :, :], v_dram[bass.ds(b, 1)].rearrange("o p t e -> p (o t) e")).then_inc(v_loaded, 16)

        def store_att(sp, b):
            for hb in range(2):
                dst = att_dram[bass.ds(b * KT, KT)].rearrange("(g two) p e -> two p g e", two=2)[hb]
                sp.dma_start(dst, att[:, hb * G:(hb + 1) * G, :]).then_inc(att_stored, 16)

        km_ready = sem("km_ready")
        sc_full = sem("sc_full")
        sc_free = sem("sc_free")
        colmax_ready = sem("colmax_ready")
        diff_ready = sem("diff_ready")
        probs_ready = sem("probs_ready")
        slot_free = sem("slot_free")
        vh_ready = sem("vh_ready")
        pv_read = sem("pv_read")
        tr_full, tr_read = sem("tr_full"), sem("tr_read")
        norm_step = sem("norm_step")

        def sync_main(sp):
            load_qk(sp, 0)
            load_v(sp, 0)
            with sp.Fori(1, B) as b:
                sp.wait_ge(sc_full, SP_FULLS * H * b)
                load_qk(sp, b)
                sp.wait_ge(vh_ready, H * b)
                load_v(sp, b)
                sp.wait_ge(att_made, H * b + START)
                store_att(sp, b - 1)
            sp.wait_ge(att_made, H * B + START)
            store_att(sp, B - 1)

        def pool_main(pool):
            pool.sem_inc(slot_free, SLOTS)
            with pool.Fori(0, NH) as n:
                pool.wait_ge(v_loaded, 16 * (n // H + 1))
                pool.wait_ge(slot_free, NCH * n + SLOTS)
                nc.gpsimd.tensor_copy(vh[:, :, 0:D], vv[:, :, bass.ds((n % H) * D, D)]).then_inc(vh_ready, 1)

        def scalar_main(act):
            act.preload_act_table(ACT.Exp)
            scale_bits = scales[0:1, :].bitcast(I32)
            scale = act.alloc_register("scale")
            with act.Fori(0, NH) as n:
                with act.Fori(0, 4) as quad:
                    for i in range(8):
                        w, half = i // 2, i % 2
                        chunk = NCH * n + 8 * quad + i
                        if i < 2:
                            act.wait_ge(diff_ready, KT * n + CK * (half + 1))
                        if half == 0:
                            act.reg_load(scale, scale_bits[:, bass.ds((4 * quad + w) * H + n % H, 1)])
                        act.wait_ge(slot_free, chunk + 1)
                        apart(act)
                        nc.scalar.activation(ring[:, i % SLOTS, :],
                                             scores[:, bass.ds(n % 2, 1), half * CK:(half + 1) * CK, :].rearrange("p o k s -> p (o k s)"),
                                             ACT.Exp, scale=scale).then_inc(probs_ready, 1)

        def score_tile(pe, m, k, first=False):
            if k == 0:
                pe.wait_ge(km_ready, m + 1)
                if not first:
                    pe.wait_ge(sc_free, SP_FREES * m)
            elif k == 1:
                if not first:
                    pe.wait_ge(diff_ready, KT * m)
            else:
                pe.wait_ge(sc_free, SP_FREES * m + k - 1)
            for half in range(2):
                cols = slice(half * HALF, (half + 1) * HALF)
                last = nc.tensor.matmul(sc[:, k % 2, cols], km[:, k * P:(k + 1) * P], qt[:, cols], start=True, stop=True)
            last.then_inc(sc_full, 1)

        def transpose_colmax(pe, m):
            pe.wait_ge(colmax_ready, m + 1)
            for t in range(KT):
                last = nc.tensor.transpose(sc[:, 0, t * P:(t + 1) * P], colmax[:, t * P:(t + 1) * P], ident[:, :])
            last.then_inc(sc_full, 1)

        def broadcast_rowmax(pe, m):
            pe.wait_ge(sc_free, SP_FREES * (m + 1))
            for t in range(KT):
                last = nc.tensor.matmul(sc[:, 1, t * P:(t + 1) * P], rowmax[:, t:t + 1].to_broadcast([P, P]),
                                        ident[:, :], start=True, stop=True)
            last.then_inc(sc_full, 1)

        def weigh_values(pe, n, w):
            bank, cols = (w // 2) % 2, slice((w % 2) * QG, (w % 2 + 1) * QG)
            if w == 0:
                pe.wait_ge(vh_ready, n + 1)
            for half in range(2):
                i = 2 * w + half
                pe.wait_ge(probs_ready, NCH * n + i + 1 + START)
                for k in range(CK):
                    for g in range(G):
                        col = k * S + g * QG
                        last = nc.tensor.matmul(pv[g * VC:(g + 1) * VC, bank, cols], vh[:, half * CK + k, :],
                                                ring[:, i % SLOTS, col:col + QG],
                                                start=(half == 0 and k == 0), stop=(half == 1 and k == CK - 1))
                last.then_inc(slot_free, 1)

        def transpose_numer(pe, n, quad):
            pe.wait_ge(tr_read, 4 * n + quad + START)
            for pair in range(2):
                pe.wait_ge(pv_read, 8 * n + 2 * quad + pair + 1)
                for blk in range(4):
                    last = nc.tensor.transpose(tr[:, pair, blk * P:(blk + 1) * P],
                                               numer[:, pair, blk * P:(blk + 1) * P], ident[:, :])
            last.then_inc(tr_full, 1)

        def head_products(pe, n, nxt):
            for quad in range(4):
                if quad == 3 and nxt is not None:
                    transpose_colmax(pe, nxt)
                for wi in range(4):
                    if quad < 2 and nxt is not None:
                        score_tile(pe, nxt, 4 * quad + wi)
                    weigh_values(pe, n, 4 * quad + wi)
                    if quad == 3 and wi == 0 and nxt is not None:
                        broadcast_rowmax(pe, nxt)
                transpose_numer(pe, n, quad)

        def tensor_main(pe):
            pe.wait_ge(qk_loaded, 32)
            for k in range(KT):
                score_tile(pe, 0, k, first=True)
            transpose_colmax(pe, 0)
            broadcast_rowmax(pe, 0)
            with pe.Fori(0, NH - 1) as n:
                head_products(pe, n, n + 1)
            head_products(pe, NH - 1, None)

        def mask_keys(dve, m, first=False):
            if not first:
                dve.wait_ge(sc_full, SP_FULLS * m - 2)
            dve.wait_ge(qk_loaded, 32 * (m // H + 1) if not first else 32)
            nc.vector.tensor_scalar(km[:, :], kt_[:, :], headmask[:, bass.ds(m % H, 1)], None, ALU.mult).then_inc(km_ready, 1)

        def copy_scores(dve, m, k):
            dve.wait_ge(sc_full, SP_FULLS * m + k + 1)
            nc.vector.tensor_copy(scores[:, bass.ds(m % 2, 1), k, :].rearrange("p o s -> p (o s)"), sc[:, k % 2, :]).then_inc(sc_free, 1)

        def column_max(dve, m, r):
            dve.wait_ge(sc_free, SP_FREES * m + KT)
            apart(dve)
            last = nc.vector.tensor_reduce(colmax[:, r * QG:(r + 1) * QG],
                                           scores[:, bass.ds(m % 2, 1), :, r * QG:(r + 1) * QG].rearrange("p o k q -> p (o q) k"),
                                           axis=AX.X, op=ALU.max)
            if r == G - 1:
                last.then_inc(colmax_ready, 1)

        def row_max(dve, m):
            dve.wait_ge(sc_full, SP_FULLS * m + KT + 1)
            nc.vector.tensor_reduce(rowmax[:, :], sc[:, 0, :].rearrange("p (t k) -> p t k", k=P), axis=AX.X,
                                    op=ALU.max).then_inc(sc_free, 1)

        def subtract_max(dve, m, k):
            if k == 0:
                dve.wait_ge(sc_full, SP_FULLS * (m + 1))
            tile_ = scores[:, bass.ds(m % 2, 1), k, :].rearrange("p o s -> p (o s)")
            nc.vector.tensor_tensor(tile_, tile_, sc[:, 1, :], ALU.subtract).then_inc(diff_ready, 1)

        def copy_numer(dve, n, quad, pair):
            dve.wait_ge(slot_free, SLOTS + NCH * n + 8 * quad + 4 * (pair + 1))
            dve.wait_ge(tr_full, 4 * n + quad + START)
            nc.vector.tensor_copy(numer[:, pair, :], pv[:, pair, :]).then_inc(pv_read, 1)

        def normalise(dve, n, quad):
            dve.wait_ge(tr_full, 4 * n + quad + 1 + START)
            blocks = tr[:, :, :].rearrange("p a (m c) -> p (a m) c", c=VC)
            nc.vector.reciprocal(recip[:, :, :].rearrange("p w t -> p (w t)"),
                                 blocks[:, :, D]).then_inc(norm_step, 1)
            dve.wait_ge(norm_step, 8 * n + 2 * quad + 1)
            nc.vector.tensor_tensor(coef[:, :, :], recip[:, :, :],
                                    wl_weight[:, 4 * quad:4 * quad + 4].rearrange("p (w o) -> p w o", o=1).to_broadcast([P, 4, 8]),
                                    ALU.mult).then_inc(norm_step, 1)
            dve.wait_ge(norm_step, 8 * n + 2 * quad + 2)
            nc.vector.tensor_tensor(parts[:, 4 * quad:4 * quad + 4, :, :].rearrange("p w t d -> p (w t) d"), blocks[:, :, 0:D],
                                    coef[:, :, :].rearrange("p w (t o) -> p (w t) o", o=1).to_broadcast([P, 32, D]),
                                    ALU.mult).then_inc(tr_read, 1)

        def sum_wavelengths(dve, n):
            dve.wait_ge(tr_read, 4 * (n + 1) + START)
            dve.wait_ge(att_stored, 32 * (n // H) + START)
            nc.vector.tensor_reduce(att[:, :, bass.ds((n % H) * D, D)], parts[:, :, :, :].rearrange("p w t d -> p t d w"),
                                    axis=AX.X, op=ALU.add).then_inc(att_made, 1)

        def vector_head(dve, n, nxt):
            if nxt is not None:
                mask_keys(dve, nxt)
                dve.wait_ge(probs_ready, NCH * n + START)
            for quad in range(4):
                for wi in range(4):
                    if nxt is not None:
                        if quad < 2:
                            copy_scores(dve, nxt, 4 * quad + wi)
                        elif quad == 2:
                            column_max(dve, nxt, wi)
                        elif wi == 0:
                            row_max(dve, nxt)
                        else:
                            for k in range(3 * (wi - 1), min(3 * wi, KT)):
                                subtract_max(dve, nxt, k)
                    if wi % 2 == 1:
                        copy_numer(dve, n, quad, wi // 2)
                normalise(dve, n, quad)
            sum_wavelengths(dve, n)

        def vector_main(dve):
            mask_keys(dve, 0, first=True)
            for k in range(KT):
                copy_scores(dve, 0, k)
            for r in range(G):
                column_max(dve, 0, r)
            row_max(dve, 0)
            for k in range(KT):
                subtract_max(dve, 0, k)
            with dve.Fori(0, NH - 1) as n:
                vector_head(dve, n, n + 1)
            vector_head(dve, NH - 1, None)

        gen_masked, gen_scores, gen_read = sem("gen_masked"), sem("gen_scores"), sem("gen_read")
        gen_step = sem("gen_step")
        gen_sine, gen_exp = sem("gen_sine"), sem("gen_exp")
        gen_angle, gen_shifted = sem("gen_angle"), sem("gen_shifted")
        gen_weighed = sem("gen_weighed")
        gen_tr, gen_tr_read, gen_pv = sem("gen_tr"), sem("gen_tr_read"), sem("gen_pv")
        g_raw, g_s, g_x, g_n, g_t, g_c = (scores[:, 0, i, :] for i in range(6))
        g_acc = scores[:, 0, 6, :]
        g_pT = scores[:, 0, 7, :]
        g_p = scores[:, 1, 0, :]
        g_max, g_neg, g_z, g_coef = (colmax[:, i:i + 1] for i in range(4))
        GEN_STEPS = 11

        def sync_general(sp):
            with sp.Fori(0, B) as b:
                sp.wait_ge(att_made, H * KT * b + START)
                load_qk(sp, b)
                load_v(sp, b)
                sp.wait_ge(att_made, H * KT * (b + 1) + START)
                store_att(sp, b)

        def tensor_general(pe):
            with pe.Fori(0, NH) as n:
                with pe.Fori(0, KT) as t:
                    j = n * KT + t
                    pe.wait_ge(gen_masked, j + 1)
                    for half in range(2):
                        cols = slice(half * HALF, (half + 1) * HALF)
                        last = nc.tensor.matmul(sc[:, 0, cols], km[:, 0:P], kt_[:, cols], start=True, stop=True)
                    last.then_inc(gen_scores, 1)
                    pe.wait_ge(gen_weighed, 2 * W * (j + 1))
                    for k in range(KT):
                        last = nc.tensor.transpose(sc[:, 1, k * P:(k + 1) * P], g_acc[:, k * P:(k + 1) * P], ident[:, :])
                    last.then_inc(gen_tr, 1)
                    pe.wait_ge(gen_tr_read, j + 1)
                    for k in range(KT):
                        last = nc.tensor.matmul(pv[:, 0, 0:D], g_pT[:, k * P:(k + 1) * P],
                                                vv[:, k, bass.ds((n % H) * D, D)], start=(k == 0), stop=(k == KT - 1))
                    last.then_inc(gen_pv, 1)

        def scalar_general(act):
            with act.Fori(0, NH * KT) as j:
                with act.Fori(0, W) as w:
                    act.wait_ge(gen_angle, j * W + w + 1)
                    nc.scalar.activation(g_c, g_t, ACT.Sin, scale=0.5).then_inc(gen_sine, 1)
                    act.wait_ge(gen_shifted, j * W + w + 1)
                    nc.scalar.activation(g_p, g_t, ACT.Exp, bias=g_neg, accum_out=g_z).then_inc(gen_exp, 1)

        def vector_general(dve):
            with dve.Fori(0, NH) as n:
                with dve.Fori(0, KT) as t:
                    j = n * KT + t
                    dve.wait_ge(qk_loaded, 32 * (n // H + 1))
                    dve.wait_ge(v_loaded, 16 * (n // H + 1))
                    dve.wait_ge(gen_scores, j + START)
                    nc.vector.tensor_scalar(km[:, 0:P], qt[:, bass.ds(t * P, P)], headmask[:, bass.ds(n % H, 1)], None,
                                            ALU.mult).then_inc(gen_masked, 1)
                    dve.wait_ge(gen_scores, j + 1 + START)
                    nc.vector.tensor_copy(g_raw, sc[:, 0, :])
                    dve.wait_ge(gen_tr, j + START)
                    nc.vector.memset(g_acc, 0.0).then_inc(gen_read, 1)
                    with dve.Fori(0, W) as w:
                        dve.wait_ge(gen_read, j + 1)
                        i = j * W + w
                        done = i * GEN_STEPS

                        nc.vector.tensor_scalar(g_s, g_raw, scales[:, bass.ds(w * H + n % H, 1)], None, ALU.mult).then_inc(gen_step, 1)
                        dve.wait_ge(gen_step, done + 1)
                        nc.vector.scalar_tensor_tensor(g_x, g_s, KERR, g_s, ALU.mult, ALU.mult).then_inc(gen_step, 1)
                        dve.wait_ge(gen_step, done + 2)
                        nc.vector.tensor_scalar(g_n, g_x, 1.0 / (2.0 * np.pi), MAGIC, ALU.mult, ALU.add).then_inc(gen_step, 1)
                        dve.wait_ge(gen_step, done + 3)
                        nc.vector.tensor_scalar(g_n, g_n, MAGIC, None, ALU.subtract).then_inc(gen_step, 1)
                        src = g_x
                        for part_no, part in enumerate(TWO_PI):
                            dve.wait_ge(gen_step, done + 4 + part_no)
                            nc.vector.scalar_tensor_tensor(g_t, g_n, -part, src, ALU.mult, ALU.add).then_inc(gen_step, 1)
                            src = g_t
                        dve.wait_ge(gen_step, done + 7)
                        nc.vector.tensor_scalar(g_t, g_t, PI, -PI, ALU.min, ALU.max).then_inc(gen_angle, 1)
                        dve.wait_ge(gen_sine, i + 1)
                        nc.vector.tensor_tensor(g_x, g_c, g_c, ALU.mult).then_inc(gen_step, 1)
                        dve.wait_ge(gen_step, done + 8)
                        nc.vector.tensor_scalar(g_x, g_x, -2.0, 1.0, ALU.mult, ALU.add).then_inc(gen_step, 1)
                        dve.wait_ge(gen_step, done + 9)
                        nc.vector.tensor_tensor(g_t, g_s, g_x, ALU.mult).then_inc(gen_step, 1)
                        dve.wait_ge(gen_step, done + 10)
                        nc.vector.tensor_reduce(g_neg, g_t, axis=AX.X, op=ALU.max, negate=True).then_inc(gen_shifted, 1)
                        dve.wait_ge(gen_exp, i + 1)
                        nc.vector.reciprocal(g_max, g_z).then_inc(gen_step, 1)
                        dve.wait_ge(gen_step, done + 11)
                        nc.vector.tensor_tensor(g_coef, g_max, wl_weight[:, bass.ds(w, 1)], ALU.mult).then_inc(gen_weighed, 1)
                        dve.wait_ge(gen_weighed, 2 * i + 1)
                        nc.vector.scalar_tensor_tensor(g_acc, g_p, g_coef, g_acc, ALU.mult, ALU.add).then_inc(gen_weighed, 1)
                        dve.wait_ge(gen_weighed, 2 * i + 2)
                        apart(dve)
                    dve.wait_ge(gen_tr, j + 1 + START)
                    nc.vector.tensor_copy(g_pT, sc[:, 1, :]).then_inc(gen_tr_read, 1)
                    dve.wait_ge(gen_pv, j + 1)
                    dve.wait_ge(att_stored, 32 * (n // H) + START)
                    nc.vector.tensor_copy(att[:, bass.ds((t % 2) * G + t // 2, 1), bass.ds((n % H) * D, D)].rearrange("p o d -> p (o d)"),
                                          pv[:, 0, 0:D]).then_inc(att_made, 1)

        weights = ring[:, :, :].rearrange("p s c -> p (s c)")
        w1_sb = weights[:, 0:NE * F].rearrange("p (e f) -> p e f", f=F)
        w2_sb = weights[:, NE * F:2 * NE * F].rearrange("p (e c d) -> p e c d", e=NE, d=E)
        pool_area = scores[:, :, :, :].rearrange("p a k s -> p (a k s)")

        def area(i, n=1):
            return pool_area[:, i * HALF:(i + n) * HALF]
        tiles = lambda a: a.rearrange("p (t e) -> p t e", e=E)
        xg, ag, aT, z, x1, x1T, z2, yo = (area(i) for i in range(8))
        hT = area(8, 2 * FC).rearrange("p (a c t) -> p a c t", a=2, t=HALF)
        stats = area(16)[:, 0:GT * 6].rearrange("p (t s) -> p t s", s=6)
        mv = area(17)[:, 0:GT * 2].rearrange("p (t s) -> p t s", s=2)
        small = area(18)
        var_, y_, t_ = small[:, 0:4], small[:, 4:8], small[:, 8:12]
        lg, ex, pr, eq, oh, oh2, gates = (small[:, 32 + 36 * i:68 + 36 * i].rearrange("p (t r) -> p t r", r=NR) for i in range(7))
        m4, s4, r4 = small[:, 300:304], small[:, 304:308], small[:, 308:312]

        ff_weights = sem("ff_weights")
        ff_in = sem("ff_in")
        ff_attT, ff_attT_made = sem("ff_attT"), sem("ff_attT_made")
        ff_y, ff_x1, ff_x1T, ff_x1T_made = sem("ff_y"), sem("ff_x1"), sem("ff_x1T"), sem("ff_x1T_made")
        ff_logits, ff_logits_made, ff_exp = sem("ff_logits"), sem("ff_logits_made"), sem("ff_exp")
        ff_hidden, ff_gelu = sem("ff_hidden"), sem("ff_gelu")
        ff_expert, ff_added = sem("ff_expert"), sem("ff_added")
        ff_step = sem("ff_step")
        ff_out, ff_stored = sem("ff_out"), sem("ff_stored")

        def sync_ff(sp):
            sp.wait_ge(att_stored, 32 * B + START)
            sp.dma_start(w1_sb, w1.rearrange("e d f -> d e f")).then_inc(ff_weights, 16)
            sp.dma_start(w2_sb.rearrange("p e c d -> p (e c) d"), w2.rearrange("e (c p) d -> p (e c) d", p=P)).then_inc(ff_weights, 16)
            with sp.Fori(0, NG) as g:
                sp.wait_ge(ff_x1, g + START)
                sp.dma_start(tiles(xg), x_tiles[bass.ds(g * GT, GT)].rearrange("t p e -> p t e")).then_inc(ff_in, 16)
                sp.dma_start(tiles(ag), att_dram[bass.ds(g * GT, GT)].rearrange("t p e -> p t e")).then_inc(ff_in, 16)
                sp.wait_ge(ff_out, g + 1)
                sp.dma_start(out_tiles[bass.ds(g * GT, GT)].rearrange("t p e -> p t e"), tiles(yo)).then_inc(ff_stored, 16)
            sp.wait_ge(ff_stored, 16 * NG + START)

        def hidden(pe, g, e):
            for c in range(FC):
                i = e * FC + c
                if i < 4:
                    pe.wait_ge(ff_gelu, NE * FC * g + START)
                else:
                    pe.wait_ge(ff_gelu, NE * FC * g + i - 3 + START)
                nc.tensor.matmul(sc[:, (i // 2) % 2, (i % 2) * HALF:(i % 2 + 1) * HALF], w1_sb[:, e, c * P:(c + 1) * P], x1T,
                                 start=True, stop=True).then_inc(ff_hidden, 1)

        def expert_out(pe, g, e):
            pe.wait_ge(ff_gelu, NE * FC * g + (e + 1) * FC + START)
            pe.wait_ge(ff_added, (NE * g + e - 1 if e >= 1 else NE * g) + START)
            for t in range(GT):
                for c in range(FC):
                    last = nc.tensor.matmul(tr[:, e % 2, t * P:(t + 1) * P], hT[:, e % 2, c, t * P:(t + 1) * P], w2_sb[:, e, c, :],
                                            start=(c == 0), stop=(c == FC - 1))
            last.then_inc(ff_expert, 1)

        def tensor_ff(pe):
            pe.wait_ge(ff_weights, 32)
            with pe.Fori(0, NG) as g:
                pe.wait_ge(ff_in, 32 * (g + 1))
                for t in range(GT):
                    last = nc.tensor.transpose(pv[:, 0, t * P:(t + 1) * P], tiles(ag)[:, t, :], ident[:, :])
                last.then_inc(ff_attT, 1)
                pe.wait_ge(ff_attT_made, g + 1)
                for t in range(GT):
                    last = nc.tensor.matmul(pv[:, 1, t * P:(t + 1) * P], aT[:, t * P:(t + 1) * P], wo_sb[:, :], start=True, stop=True)
                last.then_inc(ff_y, 1)
                pe.wait_ge(ff_x1, g + 1 + START)
                for t in range(GT):
                    last = nc.tensor.transpose(pv[:, 0, t * P:(t + 1) * P], tiles(x1)[:, t, :], ident[:, :])
                last.then_inc(ff_x1T, 1)
                pe.wait_ge(ff_x1T_made, g + 1)
                for t in range(GT):
                    last = nc.tensor.matmul(pv[:, 1, t * NR:(t + 1) * NR], x1T[:, t * P:(t + 1) * P], rw_sb[:, :], start=True, stop=True)
                last.then_inc(ff_logits, 1)
                hidden(pe, g, 0)
                for e in range(NE):
                    if e + 1 < NE:
                        hidden(pe, g, e + 1)
                    expert_out(pe, g, e)

        def scalar_ff(act):
            with act.Fori(0, NG) as g:
                act.wait_ge(ff_logits_made, g + 1)
                nc.scalar.activation(ex, lg, ACT.Exp).then_inc(ff_exp, 1)
                for i in range(NE * FC):
                    act.wait_ge(ff_hidden, NE * FC * g + i + 1)
                    if i // FC >= 2 and i % FC == 0:
                        act.wait_ge(ff_expert, NE * g + i // FC - 1 + START)
                    elif i % FC == 0:
                        act.wait_ge(ff_expert, NE * g + START)
                    nc.scalar.activation(hT[:, (i // FC) % 2, i % FC, :], sc[:, (i // 2) % 2, (i % 2) * HALF:(i % 2 + 1) * HALF],
                                         ACT.Gelu).then_inc(ff_gelu, 1)

        def vector_ff(dve):
            steps = [0]

            def body(g, total):
                def then(ins):
                    ins.then_inc(ff_step, 1)
                    steps[0] += 1
                    dve.wait_ge(ff_step, total * g + steps[0])

                def layer_norm(src, dst, signal):
                    for t in range(GT):
                        last = nc.vector.bn_stats(stats[:, t, :], tiles(src)[:, t, :])
                    then(last)
                    apart(dve)
                    for t in range(GT):
                        last = nc.vector.bn_aggr(mv[:, t, :], stats[:, t, :])
                    then(last)
                    then(nc.vector.tensor_scalar(var_, mv[:, :, 1], EPS, None, ALU.add))
                    then(nc.vector.tensor_scalar(y_.bitcast(I32), var_.bitcast(I32), -0.5, RSQRT_SEED, ALU.mult, ALU.add))
                    for _ in range(4):
                        then(nc.vector.tensor_tensor(t_, y_, y_, ALU.mult))
                        then(nc.vector.scalar_tensor_tensor(t_, t_, -0.5, var_, ALU.mult, ALU.mult))
                        then(nc.vector.scalar_tensor_tensor(y_, t_, 1.5, y_, ALU.add, ALU.mult))
                    for t in range(GT):
                        last = nc.vector.tensor_scalar(tiles(dst)[:, t, :], tiles(src)[:, t, :], mv[:, t, 0:1], y_[:, t:t + 1],
                                                       ALU.subtract, ALU.mult)
                    last.then_inc(signal, 1)

                def wide(a):
                    return a.rearrange("p (t o) -> p t o", o=1).to_broadcast([P, GT, NR])

                def pick(dst, src):
                    then(nc.vector.tensor_reduce(m4, src, axis=AX.X, op=ALU.max))
                    then(nc.vector.tensor_tensor(eq, src, wide(m4), ALU.is_equal))
                    then(nc.vector.tensor_tensor(eq, eq, rank[:, :].rearrange("p (o r) -> p o r", o=1).to_broadcast([P, GT, NR]), ALU.mult))
                    then(nc.vector.tensor_reduce(m4, eq, axis=AX.X, op=ALU.max))
                    then(nc.vector.tensor_tensor(dst, eq, wide(m4), ALU.is_equal))

                dve.wait_ge(ff_in, 32 * (g + 1))
                then(nc.vector.tensor_tensor(tiles(z), tiles(xg), bo_sb[:, :].rearrange("p (o e) -> p o e", o=1).to_broadcast([P, GT, E]), ALU.add))
                dve.wait_ge(ff_attT, g + 1)
                nc.vector.tensor_copy(aT, pv[:, 0, :]).then_inc(ff_attT_made, 1)
                dve.wait_ge(ff_y, g + 1)
                then(nc.vector.tensor_tensor(z, z, pv[:, 1, :], ALU.add))
                layer_norm(z, x1, ff_x1)
                dve.wait_ge(ff_x1T, g + 1)
                nc.vector.tensor_copy(x1T, pv[:, 0, :]).then_inc(ff_x1T_made, 1)
                dve.wait_ge(ff_logits, g + 1)
                then(nc.vector.tensor_tensor(lg, pv[:, 1, 0:GT * NR].rearrange("p (t r) -> p t r", r=NR),
                                             rb_sb[:, :].rearrange("p (o r) -> p o r", o=1).to_broadcast([P, GT, NR]), ALU.add))
                then(nc.vector.tensor_reduce(m4, lg, axis=AX.X, op=ALU.max))
                nc.vector.tensor_tensor(lg, lg, wide(m4), ALU.subtract).then_inc(ff_logits_made, 1)
                dve.wait_ge(ff_exp, g + 1)
                then(nc.vector.tensor_reduce(s4, ex, axis=AX.X, op=ALU.add))
                then(nc.vector.reciprocal(r4, s4))
                then(nc.vector.tensor_tensor(pr, ex, wide(r4), ALU.mult))
                pick(oh, pr)
                then(nc.vector.scalar_tensor_tensor(lg, oh, -2.0, pr, ALU.mult, ALU.add))
                pick(oh2, lg)
                then(nc.vector.tensor_tensor(oh, oh, oh2, ALU.add))
                then(nc.vector.tensor_tensor(gates, oh, pr, ALU.mult))
                for t in range(GT):
                    last = nc.vector.scalar_tensor_tensor(tiles(z2)[:, t, :], tiles(x1)[:, t, :], gates[:, t, NE:NE + 1],
                                                          tiles(x1)[:, t, :], ALU.mult, ALU.add)
                then(last)
                for e in range(NE):
                    dve.wait_ge(ff_expert, NE * g + e + 1 + START)
                    if e:
                        dve.wait_ge(ff_added, NE * g + e + START)
                    for t in range(GT):
                        last = nc.vector.scalar_tensor_tensor(tiles(z2)[:, t, :], tr[:, e % 2, t * P:(t + 1) * P], gates[:, t, e:e + 1],
                                                              tiles(z2)[:, t, :], ALU.mult, ALU.add)
                    last.then_inc(ff_added, 1)
                dve.wait_ge(ff_added, NE * (g + 1) + START)
                dve.wait_ge(ff_stored, 16 * g + START)
                layer_norm(z2, yo, ff_out)
                return steps[0]

            with dve.Fori(0, NG) as g:
                n = body(g, FF_STEPS)
                assert n == FF_STEPS, n
        FF_STEPS = 53

        @block.sync
        def _(sp):
            sync_setup(sp)
            sp.wait_ge(qkv_stored, 48 * B + START)
            sp.wait_ge(flag_ready, 1)
            safe = sp.value_load(flag[0:1, 0:1], min_val=0, max_val=1)
            with sp.If(safe == 1):
                sync_main(sp)
            with sp.Else():
                sync_general(sp)
            sync_ff(sp)

        @block.gpsimd
        def _(pool):
            pool_setup(pool)
            pool.wait_ge(flag_ready, 1)
            safe = pool.value_load(flag[0:1, 0:1], min_val=0, max_val=1)
            with pool.If(safe == 1):
                pool_main(pool)
            with pool.Else():
                pool.nop()

        @block.scalar
        def _(act):
            scalar_setup(act)
            act.wait_ge(flag_ready, 1)
            safe = act.value_load(flag[0:1, 0:1], min_val=0, max_val=1)
            with act.If(safe == 1):
                scalar_main(act)
            with act.Else():
                scalar_general(act)
            scalar_ff(act)

        @block.tensor
        def _(pe):
            tensor_setup(pe)
            pe.wait_ge(flag_ready, 1)
            safe = pe.value_load(flag[0:1, 0:1], min_val=0, max_val=1)
            with pe.If(safe == 1):
                tensor_main(pe)
            with pe.Else():
                tensor_general(pe)
            tensor_ff(pe)

        @block.vector
        def _(dve):
            vector_setup(dve)
            dve.wait_ge(flag_ready, 1)
            safe = dve.value_load(flag[0:1, 0:1], min_val=0, max_val=1)
            with dve.If(safe == 1):
                vector_main(dve)
            with dve.Else():
                vector_general(dve)
            vector_ff(dve)


_INS = ["L0_attn_x", "L0_attn_Wq", "L0_attn_bq", "L0_attn_Wk", "L0_attn_bk", "L0_attn_Wv", "L0_attn_bv",
        "L0_attn_Wo", "L0_attn_bo", "L0_attn_phase_modulators", "L0_attn_interference_weights",
        "L0_ffn_router_w", "L0_ffn_router_b", "L0_ffn_w1", "L0_ffn_w2"]


def kernel(**inputs):
    import concourse.bacc as bacc
    from concourse.bass_utils import run_bass_kernel_spmd

    nc = bacc.Bacc("TRN2", target_bir_lowering=False, num_devices=1)
    arrays, args = {}, []
    for name in _INS:
        a = np.ascontiguousarray(inputs[name])
        arrays[f"in_{name}"] = a
        args.append(nc.dram_tensor(f"in_{name}", a.shape, mybir.dt.from_np(a.dtype), kind="ExternalInput").ap())
    args.append(nc.dram_tensor("out", (B, S, E), FP32, kind="ExternalOutput").ap())
    build(nc, *args)
    r = run_bass_kernel_spmd(nc, [arrays], core_ids=[0])
    return r.results[0]["out"]
```

```python
from contextlib import ExitStack

import numpy as np
import concourse.bass as bass
from concourse import mybir

FP32 = mybir.dt.float32
I32 = mybir.dt.int32
ALU = mybir.AluOpType
ACT = mybir.ActivationFunctionType
AX = mybir.AxisListType

P = 128
B, S, E = 4, 1024, 128
H, D, W = 16, 8, 16
NE, F, NR = 8, 512, 9
KT = S // P
HALF = 512
NH = B * H
VC = 32
G = 4
QG = S // G
NCH = 2 * W
CK = KT // 2
SLOTS = 4
GT = 4
NG = B * S // (GT * P)
FC = F // P
TAIL = KT // GT
PAIRS = NH // 2
FIRST_PAIR = H // 2
SCALE = 1.0 / np.sqrt(D)
KERR = 2.7e-18 * 1000000.0
EPS = 1e-5
SAFE_SCORE = 9000.0
SAFE_PRODUCT = SAFE_SCORE / (SCALE * D)
MAGIC = 1.5 * 2.0 ** 23
TWO_PI = (6.28125, 0.0019352436065673828, 6.357301884918343e-08)
PI = 3.1415925
RSQRT_SEED = float(0x5F3759DF)
START = 1
SP_FULLS, SP_FREES = KT + 2, KT + 1


def build(nc, x, wq, bq, wk, bk, wv, bv, wo, bo, pm, iw, rw, rb, w1, w2, out):
    qt_dram = nc.dram_tensor("qt_scratch", (B, P, S), FP32, kind="Internal").ap()
    kt_dram = nc.dram_tensor("kt_scratch", (B, P, S), FP32, kind="Internal").ap()
    v_dram = nc.dram_tensor("v_scratch", (B, P, KT, E), FP32, kind="Internal").ap()
    att_dram = nc.dram_tensor("att_scratch", (B * S // P, P, E), FP32, kind="Internal").ap()
    x_tiles = x.rearrange("b (t p) e -> (b t) p e", p=P)
    out_tiles = out.rearrange("b (t p) e -> (b t) p e", p=P)

    ctx = ExitStack()
    with ctx:
        def sb(name, shape, dt=FP32):
            return ctx.enter_context(nc.sbuf_tensor(name, shape, dt))

        def ps(name, shape):
            return ctx.enter_context(nc.psum_tensor(name, shape, FP32))

        def sem(name):
            return ctx.enter_context(nc.semaphore(name))

        ident = sb("ident", [P, P])
        headmask = sb("headmask", [P, H])
        rank = sb("rank", [P, NR])
        scales = sb("scales", [P, W * H])
        pm_sb = sb("pm_sb", [P, W * H])
        trig = sb("trig", [P, W * H])
        wl_weight = sb("wl_weight", [P, W])
        wq_sb, wk_sb, wv_sb, wo_sb = (sb(n, [P, E]) for n in ("wq_sb", "wk_sb", "wv_sb", "wo_sb"))
        bq_sb, bk_sb = sb("bq_sb", [P, 1]), sb("bk_sb", [P, 1])
        bv_sb, bo_sb = sb("bv_sb", [P, E]), sb("bo_sb", [P, E])
        rw_sb, rb_sb = sb("rw_sb", [P, NR]), sb("rb_sb", [P, NR])
        peak = sb("peak", [P, 2 * B])
        peak_row = sb("peak_row", [1, 2])
        product = sb("product", [1, 1])
        flag = sb("flag", [1, 1], I32)

        qt = sb("qt", [P, S])
        kt_ = sb("kt_", [P, S])
        vv = sb("vv", [P, KT, E])
        km = sb("km", [P, S])
        scores = sb("scores", [P, 2, KT, S])
        ring = sb("ring", [P, SLOTS, CK * S])
        vh = sb("vh", [P, KT, VC])
        colmax = sb("colmax", [P, S])
        rowmax = sb("rowmax", [P, KT])
        numer = sb("numer", [P, 2, HALF])
        recip = sb("recip", [P, 4, 8])
        coef = sb("coef", [P, 4, 8])
        parts = sb("parts", [P, W, 8, D])
        att = sb("att", [P, KT, E])

        tile_w = sb("tile_w", [P, NE * F])
        tile_h = sb("tile_h", [P, NE * F])
        tile_x, tile_att, tile_attT, tile_z, tile_x1, tile_x1T, tile_out = (
            sb(n, [P, E]) for n in ("tile_x", "tile_att", "tile_attT", "tile_z", "tile_x1", "tile_x1T", "tile_out"))
        tile_small = sb("tile_small", [P, 96])

        pv = ps("pv", [P, 2, HALF])
        tr = ps("tr", [P, 2, HALF])
        sc = ps("sc", [P, 2, S])

        consts_loaded = sem("consts_loaded")
        consts_made = sem("consts_made")
        mask_zeroed = sem("mask_zeroed")
        flag_ready = sem("flag_ready")

        block = ctx.enter_context(nc.Block())

        def apart(engine):
            engine.nop(nofuse=True)

        scale_step = sem("scale_step")
        sine_ready = sem("sine_ready")
        x_loaded = sem("x_loaded")
        xT_ready, xT_made = sem("xT_ready"), sem("xT_made")
        q_mm, k_mm, v_mm = sem("q_mm"), sem("k_mm"), sem("v_mm")
        q_made, k_made, v_made = sem("q_made"), sem("k_made"), sem("v_made")
        peak_made = sem("peak_made")
        qkv_stored = sem("qkv_stored")
        peak_rows, peak_step = sem("peak_rows"), sem("peak_step")
        xa = scores[:, 0, 0, :].rearrange("p (t e) -> p t e", e=E)
        xT = scores[:, 0, 1, :]
        CONST_DMAS = 12

        def sync_setup(sp):
            def everywhere(ap, n):
                return ap.rearrange("(o n) -> o n", o=1).to_broadcast([P, n])
            loads = [(wq_sb[:, :], wq), (wk_sb[:, :], wk), (wv_sb[:, :], wv), (wo_sb[:, :], wo),
                     (bq_sb[:, :], bq.rearrange("(p o) -> p o", o=1)),
                     (bk_sb[:, :], bk.rearrange("(p o) -> p o", o=1)),
                     (bv_sb[:, :], everywhere(bv, E)), (bo_sb[:, :], everywhere(bo, E)),
                     (rw_sb[:, :], rw), (rb_sb[:, :], everywhere(rb, NR)),
                     (pm_sb[:, :], everywhere(pm.rearrange("w h -> (w h)"), W * H)),
                     (wl_weight[:, :], everywhere(iw, W))]
            for dst, src in loads:
                sp.dma_start(dst, src).then_inc(consts_loaded, 16)
            with sp.Fori(0, B) as b:
                sp.wait_ge(xT_ready, b + START)
                sp.dma_start(xa, x_tiles[bass.ds(b * KT, KT)].rearrange("t p e -> p t e")).then_inc(x_loaded, 16)
                sp.wait_ge(q_made, b + 1 + START)
                sp.dma_start(qt_dram[bass.ds(b, 1)].rearrange("o p s -> p (o s)"), qt[:, :]).then_inc(qkv_stored, 16)
                sp.wait_ge(k_made, b + 1 + START)
                sp.dma_start(kt_dram[bass.ds(b, 1)].rearrange("o p s -> p (o s)"), kt_[:, :]).then_inc(qkv_stored, 16)
                sp.wait_ge(v_made, b + 1 + START)
                sp.dma_start(v_dram[bass.ds(b, 1)].rearrange("o p t e -> p (o t) e"), vv[:, :, :]).then_inc(qkv_stored, 16)

        def pool_setup(pool):
            for started in (xT_ready, q_made, k_made, v_mm, v_made, peak_made, qkv_stored, probs_ready, tr_full,
                            tr_read, att_made, att_stored, gen_scores, gen_tr, ff_x1, ff_gelu, ff_expert,
                            ff_added, ff_stored, tile_x1_made, tile_products, tile_out_free):
                pool.sem_inc(started, START)
            nc.gpsimd.memset(ident[:, :], 1.0)
            nc.gpsimd.memset(headmask[:, :], 1.0)
            for e in range(NR):
                nc.gpsimd.memset(rank[:, e:e + 1], float(NR - e))
            nc.gpsimd.memset(vh[:, :, :], 0.0).then_inc(mask_zeroed, 1)
            pool.wait_ge(mask_zeroed, 1)
            nc.gpsimd.memset(vh[:, :, D:D + 1], 1.0)
            nc.gpsimd.affine_select(out=ident[:, :], in_=ident[:, :], compare_op=ALU.is_equal, fill=0.0,
                                    base=0, pattern=[[-1, P]], channel_multiplier=1)
            nc.gpsimd.affine_select(out=headmask[:, :], in_=headmask[:, :], compare_op=ALU.is_ge, fill=0.0,
                                    base=0, pattern=[[-D, H]], channel_multiplier=1).then_inc(mask_zeroed, 1)
            pool.wait_ge(mask_zeroed, 2)
            nc.gpsimd.affine_select(out=headmask[:, :], in_=headmask[:, :], compare_op=ALU.is_ge, fill=0.0,
                                    base=D - 1, pattern=[[D, H]], channel_multiplier=-1).then_inc(consts_made, 1)

        def scalar_setup(act):
            act.wait_ge(scale_step, 5)
            nc.scalar.activation(trig[:, :], trig[:, :], ACT.Sin, scale=0.5).then_inc(sine_ready, 1)
            act.wait_ge(consts_loaded, 16 * CONST_DMAS)
            act.preload_act_table(ACT.Exp)
            with act.Fori(0, B) as b:
                act.wait_ge(q_mm, b + 1)
                act.wait_ge(qkv_stored, 48 * b + START)
                act.wait_ge(peak_made, b + START)
                nc.scalar.activation(qt[:, :], sc[:, 1, :], ACT.Identity, bias=bq_sb[:, 0:1]).then_inc(q_made, 1)
                act.wait_ge(k_mm, b + 1)
                nc.scalar.activation(kt_[:, :], sc[:, 0, :], ACT.Identity, bias=bk_sb[:, 0:1]).then_inc(k_made, 1)

        def tensor_setup(pe):
            pe.wait_ge(consts_made, 1)
            pe.wait_ge(consts_loaded, 16 * CONST_DMAS)
            with pe.Fori(0, B) as b:
                pe.wait_ge(x_loaded, 16 * (b + 1))
                pe.wait_ge(k_made, b + START)
                for t in range(KT):
                    last = nc.tensor.transpose(sc[:, 0, t * P:(t + 1) * P], xa[:, t, :], ident[:, :])
                last.then_inc(xT_ready, 1)
                pe.wait_ge(xT_made, b + 1)
                pe.wait_ge(q_made, b + START)
                for half in range(2):
                    cols = slice(half * HALF, (half + 1) * HALF)
                    last = nc.tensor.matmul(sc[:, 1, cols], wq_sb[:, :], xT[:, cols], start=True, stop=True)
                last.then_inc(q_mm, 1)
                for half in range(2):
                    cols = slice(half * HALF, (half + 1) * HALF)
                    last = nc.tensor.matmul(sc[:, 0, cols], wk_sb[:, :], xT[:, cols], start=True, stop=True)
                last.then_inc(k_mm, 1)
                pe.wait_ge(v_made, b + START)
                for t in range(KT):
                    last = nc.tensor.matmul(tr[:, t // 4, (t % 4) * P:(t % 4 + 1) * P], xT[:, t * P:(t + 1) * P],
                                            wv_sb[:, :], start=True, stop=True)
                last.then_inc(v_mm, 1)
            pe.wait_ge(peak_step, 1)
            for i in range(2):
                last = nc.tensor.matmul(pv[0:1, 0, i * P:(i + 1) * P], peak[:, i:i + 1], ident[:, :],
                                        start=True, stop=True)
            last.then_inc(peak_rows, 1)

        def vector_setup(dve):
            dve.wait_ge(consts_loaded, 16 * CONST_DMAS)
            whole = colmax[:, 0:W * H]
            nc.vector.tensor_scalar(wl_weight[:, :], wl_weight[:, :], 1.0 / W, None, ALU.mult)
            nc.vector.tensor_scalar(whole, pm_sb[:, :], 1.0 / (2.0 * np.pi), MAGIC, ALU.mult, ALU.add).then_inc(scale_step, 1)
            dve.wait_ge(scale_step, 1)
            nc.vector.tensor_scalar(whole, whole, MAGIC, None, ALU.subtract).then_inc(scale_step, 1)
            src = pm_sb[:, :]
            for i, part in enumerate(TWO_PI):
                dve.wait_ge(scale_step, 2 + i)
                nc.vector.scalar_tensor_tensor(trig[:, :], whole, -part, src, ALU.mult, ALU.add).then_inc(scale_step, 1)
                src = trig[:, :]
            dve.wait_ge(sine_ready, 1)
            nc.vector.tensor_tensor(pm_sb[:, :], trig[:, :], trig[:, :], ALU.mult).then_inc(scale_step, 1)
            dve.wait_ge(scale_step, 6)
            nc.vector.tensor_scalar(trig[:, :], pm_sb[:, :], -2.0, 1.0, ALU.mult, ALU.add).then_inc(scale_step, 1)
            dve.wait_ge(scale_step, 7)
            nc.vector.tensor_tensor(pm_sb[:, :], trig[:, :], trig[:, :], ALU.mult).then_inc(scale_step, 1)
            dve.wait_ge(scale_step, 8)
            nc.vector.tensor_scalar(scales[:, :], pm_sb[:, :], SCALE, None, ALU.mult).then_inc(scale_step, 1)
            with dve.Fori(0, B) as b:
                dve.wait_ge(xT_ready, b + 1 + START)
                dve.wait_ge(v_mm, b + START)
                nc.vector.tensor_copy(xT, sc[:, 0, :]).then_inc(xT_made, 1)
                dve.wait_ge(v_mm, b + 1 + START)
                dve.wait_ge(qkv_stored, 48 * b + START)
                nc.vector.tensor_tensor(vv[:, :, :], tr[:, :, :].rearrange("p a (t e) -> p (a t) e", e=E),
                                        bv_sb[:, :].rearrange("p (o e) -> p o e", o=1).to_broadcast([P, KT, E]),
                                        ALU.add).then_inc(v_made, 1)
                dve.wait_ge(q_made, b + 1 + START)
                nc.vector.tensor_reduce(peak[:, bass.ds(b, 1)], qt[:, :], axis=AX.X, op=ALU.max,
                                        apply_absolute_value=True)
                dve.wait_ge(k_made, b + 1 + START)
                nc.vector.tensor_reduce(peak[:, bass.ds(b + B, 1)], kt_[:, :], axis=AX.X, op=ALU.max,
                                        apply_absolute_value=True).then_inc(peak_made, 1)
            dve.wait_ge(peak_made, B + START)
            nc.vector.tensor_reduce(recip[:, 0, 0:2], peak[:, :].rearrange("p (i b) -> p i b", b=B), axis=AX.X, op=ALU.max).then_inc(peak_made, 1)
            dve.wait_ge(peak_made, B + 1 + START)
            nc.vector.tensor_copy(peak[:, 0:2], recip[:, 0, 0:2]).then_inc(peak_step, 1)
            dve.wait_ge(peak_rows, 1)
            nc.vector.tensor_reduce(peak_row[:, :], pv[0:1, 0, 0:2 * P].rearrange("p (i q) -> p i q", q=P), axis=AX.X,
                                    op=ALU.max).then_inc(peak_step, 1)
            dve.wait_ge(peak_step, 2)
            nc.vector.tensor_tensor(product[:, :], peak_row[:, 0:1], peak_row[:, 1:2], ALU.mult).then_inc(peak_step, 1)
            dve.wait_ge(peak_step, 3)
            nc.vector.tensor_scalar(flag[:, :], product[:, :], SAFE_PRODUCT, None, ALU.is_lt).then_inc(flag_ready, 1)

        def stepper(dve, signal, base, counted):
            def then(ins):
                ins.then_inc(signal, 1)
                counted[0] += 1
                dve.wait_ge(signal, base + counted[0])
            return then

        def over_tiles(row, nt):
            n = row.shape[1]
            return row[:, :].rearrange("p (o n) -> p o n", o=1).to_broadcast([P, nt, n])

        def wide(a, nt):
            return a.rearrange("p (t o) -> p t o", o=1).to_broadcast([P, nt, NR])

        def norm_views(a, nt):
            cols = [a[:, i * nt:(i + 1) * nt] for i in range(8, 11)]
            return (a[:, 0:6 * nt].rearrange("p (t s) -> p t s", s=6), a[:, 6 * nt:8 * nt].rearrange("p (t s) -> p t s", s=2), *cols)

        def route_views(a, nt):
            return [a[:, i * NR * nt:(i + 1) * NR * nt].rearrange("p (t r) -> p t r", r=NR) for i in range(7)]

        def layer_norm(then, src, dst, nt, views, dve):
            stats, mv, var_, y_, t_ = views
            src, dst = (a.rearrange("p (t e) -> p t e", e=E) for a in (src, dst))
            for t in range(nt):
                last = nc.vector.bn_stats(stats[:, t, :], src[:, t, :])
            then(last)
            apart(dve)
            for t in range(nt):
                last = nc.vector.bn_aggr(mv[:, t, :], stats[:, t, :])
            then(last)
            then(nc.vector.tensor_scalar(var_, mv[:, :, 1], EPS, None, ALU.add))
            then(nc.vector.tensor_scalar(y_.bitcast(I32), var_.bitcast(I32), -0.5, RSQRT_SEED, ALU.mult, ALU.add))
            for _ in range(4):
                then(nc.vector.tensor_tensor(t_, y_, y_, ALU.mult))
                then(nc.vector.scalar_tensor_tensor(t_, t_, -0.5, var_, ALU.mult, ALU.mult))
                then(nc.vector.scalar_tensor_tensor(y_, t_, 1.5, y_, ALU.add, ALU.mult))
            for t in range(nt):
                last = nc.vector.tensor_scalar(dst[:, t, :], src[:, t, :], mv[:, t, 0:1], y_[:, t:t + 1], ALU.subtract, ALU.mult)
            return last

        def route(then, views, four, nt):
            lg, ex, pr, eq, oh, oh2, gates = views
            m4, s4, r4 = four

            def pick(dst, src):
                then(nc.vector.tensor_reduce(m4, src, axis=AX.X, op=ALU.max))
                then(nc.vector.tensor_tensor(eq, src, wide(m4, nt), ALU.is_equal))
                then(nc.vector.tensor_tensor(eq, eq, over_tiles(rank, nt), ALU.mult))
                then(nc.vector.tensor_reduce(m4, eq, axis=AX.X, op=ALU.max))
                then(nc.vector.tensor_tensor(dst, eq, wide(m4, nt), ALU.is_equal))

            then(nc.vector.tensor_reduce(s4, ex, axis=AX.X, op=ALU.add))
            then(nc.vector.reciprocal(r4, s4))
            then(nc.vector.tensor_tensor(pr, ex, wide(r4, nt), ALU.mult))
            pick(oh, pr)
            then(nc.vector.scalar_tensor_tensor(lg, oh, -2.0, pr, ALU.mult, ALU.add))
            pick(oh2, lg)
            then(nc.vector.tensor_tensor(oh, oh, oh2, ALU.add))
            then(nc.vector.tensor_tensor(gates, oh, pr, ALU.mult))

        t_norm = norm_views(tile_small, 1)
        t_route = route_views(tile_small[:, 11:11 + 7 * NR], 1)
        t_lg, t_ex = t_route[0], t_route[1]
        t_four = [tile_small[:, i:i + 1] for i in range(74, 77)]

        qk_loaded, v_loaded = sem("qk_loaded"), sem("v_loaded")
        att_made, att_stored = sem("att_made"), sem("att_stored")

        def load_qk(sp, b):
            sp.dma_start(qt[:, :], qt_dram[bass.ds(b, 1)].rearrange("o p s -> p (o s)")).then_inc(qk_loaded, 16)
            sp.dma_start(kt_[:, :], kt_dram[bass.ds(b, 1)].rearrange("o p s -> p (o s)")).then_inc(qk_loaded, 16)

        def load_v(sp, b):
            sp.dma_start(vv[:, :, :], v_dram[bass.ds(b, 1)].rearrange("o p t e -> p (o t) e")).then_inc(v_loaded, 16)

        def store_att(sp, b):
            for hb in range(2):
                dst = att_dram[bass.ds(b * KT, KT)].rearrange("(g two) p e -> two p g e", two=2)[hb]
                sp.dma_start(dst, att[:, hb * G:(hb + 1) * G, :]).then_inc(att_stored, 16)

        km_ready = sem("km_ready")
        sc_full = sem("sc_full")
        sc_free = sem("sc_free")
        colmax_ready = sem("colmax_ready")
        diff_ready = sem("diff_ready")
        probs_ready = sem("probs_ready")
        slot_free = sem("slot_free")
        vh_ready = sem("vh_ready")
        pv_read = sem("pv_read")
        tr_full, tr_read = sem("tr_full"), sem("tr_read")
        norm_step = sem("norm_step")
        tile_in, tile_w1, tile_w2 = sem("tile_in"), sem("tile_w1"), sem("tile_w2")
        tile_attT_ready, tile_attT_made, tile_y = sem("tile_attT_ready"), sem("tile_attT_made"), sem("tile_y")
        tile_x1_made, tile_x1T_ready, tile_x1T_made = sem("tile_x1_made"), sem("tile_x1T_ready"), sem("tile_x1T_made")
        tile_logits, tile_logits_made, tile_exp = sem("tile_logits"), sem("tile_logits_made"), sem("tile_exp")
        tile_hidden, tile_hidden_copied = sem("tile_hidden"), sem("tile_hidden_copied")
        tile_gelu, tile_products, tile_added = sem("tile_gelu"), sem("tile_products"), sem("tile_added")
        tile_step, tile_done, tile_stored, tile_out_free = (
            sem("tile_step"), sem("tile_done"), sem("tile_stored"), sem("tile_out_free"))

        def sync_main(sp):
            load_qk(sp, 0)
            load_v(sp, 0)
            with sp.Fori(1, B) as b:
                sp.wait_ge(sc_full, SP_FULLS * H * b)
                load_qk(sp, b)
                sp.wait_ge(vh_ready, H * b)
                load_v(sp, b)
                sp.wait_ge(att_made, H * b + START)
                store_att(sp, b - 1)
                sp.wait_ge(att_stored, 32 * b + START)
                apart(sp)
                with sp.Fori(0, KT) as t:
                    i = (b - 1) * KT + t
                    sp.wait_ge(tile_x1_made, i + START)
                    sp.dma_start(tile_x[:, :], x_tiles[bass.ds(i, 1)].rearrange("o p e -> p (o e)")).then_inc(tile_in, 16)
                    sp.dma_start(tile_att[:, :], att_dram[bass.ds(i, 1)].rearrange("o p e -> p (o e)")).then_inc(tile_in, 16)
                    sp.wait_ge(tile_products, i + START)
                    sp.dma_start(tile_w[:, :], w1.rearrange("d e f -> d (e f)")).then_inc(tile_w1, 16)
                    sp.wait_ge(tile_hidden, 4 * (i + 1))
                    sp.dma_start(tile_w[:, :], w2.rearrange("p e c d -> p (e c d)")).then_inc(tile_w2, 16)
            sp.wait_ge(att_made, H * B + START)
            store_att(sp, B - 1)

        def copy_values(pool, n):
            pool.wait_ge(v_loaded, 16 * (n // H + 1))
            pool.wait_ge(slot_free, NCH * n + SLOTS)
            nc.gpsimd.tensor_copy(vh[:, :, 0:D], vv[:, :, bass.ds((n % H) * D, D)]).then_inc(vh_ready, 1)

        def pool_main(pool):
            pool.sem_inc(slot_free, SLOTS)
            with pool.Fori(0, H) as n:
                copy_values(pool, n)
            with pool.Fori(0, PAIRS - FIRST_PAIR) as i:
                copy_values(pool, 2 * (i + FIRST_PAIR))
                copy_values(pool, 2 * (i + FIRST_PAIR) + 1)
                pool.wait_ge(tile_done, i + 1)
                pool.dma_start(out_tiles[bass.ds(i, 1)].rearrange("o p e -> p (o e)"), tile_out[:, :]).then_inc(tile_stored, 16)
                pool.wait_ge(tile_stored, 16 * (i + 1))
                pool.sem_inc(tile_out_free, 1)

        def scalar_main(act):
            act.preload_act_table(ACT.Exp)
            scale_bits = scales[0:1, :].bitcast(I32)
            scale = act.alloc_register("scale")

            def quads(n, first, last):
                with act.Fori(first, last) as quad:
                    for i in range(8):
                        w, half = i // 2, i % 2
                        chunk = NCH * n + 8 * quad + i
                        if i < 2:
                            act.wait_ge(diff_ready, KT * n + CK * (half + 1))
                        if half == 0:
                            act.reg_load(scale, scale_bits[:, bass.ds((4 * quad + w) * H + n % H, 1)])
                        act.wait_ge(slot_free, chunk + 1)
                        apart(act)
                        nc.scalar.activation(ring[:, i % SLOTS, :],
                                             scores[:, bass.ds(n % 2, 1), half * CK:(half + 1) * CK, :].rearrange("p o k s -> p (o k s)"),
                                             ACT.Exp, scale=scale).then_inc(probs_ready, 1)

            with act.Fori(0, H) as n:
                quads(n, 0, 4)
            with act.Fori(0, PAIRS - FIRST_PAIR) as i:
                n = 2 * (i + FIRST_PAIR)
                quads(n, 0, 3)
                act.wait_ge(tile_logits_made, i + 1)
                nc.scalar.activation(t_ex, t_lg, ACT.Exp).then_inc(tile_exp, 1)
                quads(n, 3, 4)
                quads(n + 1, 0, 1)
                act.wait_ge(tile_hidden_copied, 4 * (i + 1))
                nc.scalar.activation(tile_h[:, :], tile_h[:, :], ACT.Gelu).then_inc(tile_gelu, 1)
                act.preload_act_table(ACT.Exp)
                quads(n + 1, 1, 4)

        def score_tile(pe, m, k, first=False):
            if k == 0:
                pe.wait_ge(km_ready, m + 1)
                if not first:
                    pe.wait_ge(sc_free, SP_FREES * m)
            elif k == 1:
                if not first:
                    pe.wait_ge(diff_ready, KT * m)
            else:
                pe.wait_ge(sc_free, SP_FREES * m + k - 1)
            for half in range(2):
                cols = slice(half * HALF, (half + 1) * HALF)
                last = nc.tensor.matmul(sc[:, k % 2, cols], km[:, k * P:(k + 1) * P], qt[:, cols], start=True, stop=True)
            last.then_inc(sc_full, 1)

        def transpose_colmax(pe, m, tile_no=None):
            pe.wait_ge(colmax_ready, m + 1)
            if tile_no is not None:
                pe.wait_ge(tile_hidden_copied, 4 * tile_no + 3)
            for t in range(KT):
                last = nc.tensor.transpose(sc[:, 0, t * P:(t + 1) * P], colmax[:, t * P:(t + 1) * P], ident[:, :])
            last.then_inc(sc_full, 1)

        def broadcast_rowmax(pe, m, slot_read=None):
            pe.wait_ge(sc_free, SP_FREES * (m + 1))
            if slot_read is not None:
                pe.wait_ge(*slot_read)
            for t in range(KT):
                last = nc.tensor.matmul(sc[:, 1, t * P:(t + 1) * P], rowmax[:, t:t + 1].to_broadcast([P, P]),
                                        ident[:, :], start=True, stop=True)
            last.then_inc(sc_full, 1)

        def weigh_values(pe, n, w):
            bank, cols = (w // 2) % 2, slice((w % 2) * QG, (w % 2 + 1) * QG)
            if w == 0:
                pe.wait_ge(vh_ready, n + 1)
            for half in range(2):
                i = 2 * w + half
                pe.wait_ge(probs_ready, NCH * n + i + 1 + START)
                for k in range(CK):
                    for g in range(G):
                        col = k * S + g * QG
                        last = nc.tensor.matmul(pv[g * VC:(g + 1) * VC, bank, cols], vh[:, half * CK + k, :],
                                                ring[:, i % SLOTS, col:col + QG],
                                                start=(half == 0 and k == 0), stop=(half == 1 and k == CK - 1))
                last.then_inc(slot_free, 1)

        def transpose_numer(pe, n, quad):
            pe.wait_ge(tr_read, 4 * n + quad + START)
            for pair in range(2):
                pe.wait_ge(pv_read, 8 * n + 2 * quad + pair + 1)
                for blk in range(4):
                    last = nc.tensor.transpose(tr[:, pair, blk * P:(blk + 1) * P],
                                               numer[:, pair, blk * P:(blk + 1) * P], ident[:, :])
            last.then_inc(tr_full, 1)

        def tile_part_one(pe, i, m, wi):
            if wi == 0:
                pe.wait_ge(tile_in, 32 * (i + 1))
                pe.wait_ge(sc_free, SP_FREES * m + KT)
                nc.tensor.transpose(sc[:, 0, 0:P], tile_att[:, :], ident[:, :]).then_inc(tile_attT_ready, 1)
            elif wi == 1:
                pe.wait_ge(tile_attT_made, i + 1)
                nc.tensor.matmul(sc[:, 1, 0:E], tile_attT[:, :], wo_sb[:, :], start=True, stop=True).then_inc(tile_y, 1)
            elif wi == 2:
                pe.wait_ge(tile_x1_made, i + 1 + START)
                nc.tensor.transpose(sc[:, 0, 0:P], tile_x1[:, :], ident[:, :]).then_inc(tile_x1T_ready, 1)
            elif wi == 3:
                pe.wait_ge(tile_x1T_made, i + 1)
                nc.tensor.matmul(sc[:, 1, 0:NR], tile_x1T[:, :], rw_sb[:, :], start=True, stop=True).then_inc(tile_logits, 1)
                tile_slice(pe, i, 0)

        def tile_slice(pe, i, k):
            if k == 0:
                pe.wait_ge(tile_w1, 16 * (i + 1))
            elif k == 1:
                pe.wait_ge(tile_logits_made, i + 1)
            else:
                pe.wait_ge(tile_hidden_copied, 4 * i + k - 1)
            for j in range(2 * FC):
                col = (2 * FC * k + j) * P
                last = nc.tensor.matmul(sc[:, k % 2, j * P:(j + 1) * P], tile_w[:, col:col + P], tile_x1T[:, :], start=True, stop=True)
            last.then_inc(tile_hidden, 1)

        def tile_part_two(pe, i, nxt, wi):
            if wi == 0:
                pe.wait_ge(tile_w2, 16 * (i + 1))
                pe.wait_ge(tile_gelu, i + 1)
                if nxt is not None:
                    pe.wait_ge(sc_free, SP_FREES * nxt + KT)
                else:
                    pe.wait_ge(diff_ready, KT * NH)
            for e in (2 * wi, 2 * wi + 1):
                for c in range(FC):
                    col = (e * FC + c) * P
                    last = nc.tensor.matmul(sc[:, 1, e * P:(e + 1) * P], tile_h[:, col:col + P], tile_w[:, col:col + P],
                                            start=(c == 0), stop=(c == FC - 1))
            if wi == 3:
                last.then_inc(tile_products, 1)

        def head_products(pe, n, nxt, tile_no=None, part=0):
            for quad in range(4):
                if quad == 3 and nxt is not None:
                    transpose_colmax(pe, nxt, tile_no if part == 1 else None)
                for wi in range(4):
                    if quad < 2 and nxt is not None:
                        score_tile(pe, nxt, 4 * quad + wi)
                    if quad == 2 and part == 1:
                        tile_part_one(pe, tile_no, nxt, wi)
                    weigh_values(pe, n, 4 * quad + wi)
                    if quad == 2 and part == 2:
                        tile_part_two(pe, tile_no, nxt, wi)
                    if quad == 3 and wi == 0 and nxt is not None:
                        broadcast_rowmax(pe, nxt, [None, (tile_hidden_copied, 4 * tile_no + 4), (tile_added, tile_no + 1)][part]
                                         if part else None)
                if quad == 2 and part == 1:
                    for k in range(1, 4):
                        tile_slice(pe, tile_no, k)
                transpose_numer(pe, n, quad)

        def tensor_main(pe):
            pe.wait_ge(qk_loaded, 32)
            for k in range(KT):
                score_tile(pe, 0, k, first=True)
            transpose_colmax(pe, 0)
            broadcast_rowmax(pe, 0)
            with pe.Fori(0, H) as n:
                head_products(pe, n, n + 1)
            with pe.Fori(0, PAIRS - FIRST_PAIR - 1) as i:
                n = 2 * (i + FIRST_PAIR)
                head_products(pe, n, n + 1, i, 1)
                head_products(pe, n + 1, n + 2, i, 2)
            head_products(pe, NH - 2, NH - 1, PAIRS - FIRST_PAIR - 1, 1)
            head_products(pe, NH - 1, None, PAIRS - FIRST_PAIR - 1, 2)

        def mask_keys(dve, m, first=False):
            if not first:
                dve.wait_ge(sc_full, SP_FULLS * m - 2)
            dve.wait_ge(qk_loaded, 32 * (m // H + 1) if not first else 32)
            nc.vector.tensor_scalar(km[:, :], kt_[:, :], headmask[:, bass.ds(m % H, 1)], None, ALU.mult).then_inc(km_ready, 1)

        def copy_scores(dve, m, k):
            dve.wait_ge(sc_full, SP_FULLS * m + k + 1)
            nc.vector.tensor_copy(scores[:, bass.ds(m % 2, 1), k, :].rearrange("p o s -> p (o s)"), sc[:, k % 2, :]).then_inc(sc_free, 1)

        def column_max(dve, m, r):
            dve.wait_ge(sc_free, SP_FREES * m + KT)
            apart(dve)
            last = nc.vector.tensor_reduce(colmax[:, r * QG:(r + 1) * QG],
                                           scores[:, bass.ds(m % 2, 1), :, r * QG:(r + 1) * QG].rearrange("p o k q -> p (o q) k"),
                                           axis=AX.X, op=ALU.max)
            if r == G - 1:
                last.then_inc(colmax_ready, 1)

        def row_max(dve, m):
            dve.wait_ge(sc_full, SP_FULLS * m + KT + 1)
            nc.vector.tensor_reduce(rowmax[:, :], sc[:, 0, :].rearrange("p (t k) -> p t k", k=P), axis=AX.X,
                                    op=ALU.max).then_inc(sc_free, 1)

        def subtract_max(dve, m, k):
            if k == 0:
                dve.wait_ge(sc_full, SP_FULLS * (m + 1))
            tile_ = scores[:, bass.ds(m % 2, 1), k, :].rearrange("p o s -> p (o s)")
            nc.vector.tensor_tensor(tile_, tile_, sc[:, 1, :], ALU.subtract).then_inc(diff_ready, 1)

        def copy_numer(dve, n, quad, pair):
            dve.wait_ge(slot_free, SLOTS + NCH * n + 8 * quad + 4 * (pair + 1))
            dve.wait_ge(tr_full, 4 * n + quad + START)
            nc.vector.tensor_copy(numer[:, pair, :], pv[:, pair, :]).then_inc(pv_read, 1)

        def normalise(dve, n, quad):
            dve.wait_ge(tr_full, 4 * n + quad + 1 + START)
            blocks = tr[:, :, :].rearrange("p a (m c) -> p (a m) c", c=VC)
            nc.vector.reciprocal(recip[:, :, :].rearrange("p w t -> p (w t)"),
                                 blocks[:, :, D]).then_inc(norm_step, 1)
            dve.wait_ge(norm_step, 8 * n + 2 * quad + 1)
            nc.vector.tensor_tensor(coef[:, :, :], recip[:, :, :],
                                    wl_weight[:, 4 * quad:4 * quad + 4].rearrange("p (w o) -> p w o", o=1).to_broadcast([P, 4, 8]),
                                    ALU.mult).then_inc(norm_step, 1)
            dve.wait_ge(norm_step, 8 * n + 2 * quad + 2)
            nc.vector.tensor_tensor(parts[:, 4 * quad:4 * quad + 4, :, :].rearrange("p w t d -> p (w t) d"), blocks[:, :, 0:D],
                                    coef[:, :, :].rearrange("p w (t o) -> p (w t) o", o=1).to_broadcast([P, 32, D]),
                                    ALU.mult).then_inc(tr_read, 1)

        def sum_wavelengths(dve, n):
            dve.wait_ge(tr_read, 4 * (n + 1) + START)
            dve.wait_ge(att_stored, 32 * (n // H) + START)
            nc.vector.tensor_reduce(att[:, :, bass.ds((n % H) * D, D)], parts[:, :, :, :].rearrange("p w t d -> p t d w"),
                                    axis=AX.X, op=ALU.add).then_inc(att_made, 1)

        def tile_part_one_vector(dve, i, wi, then):
            if wi == 0:
                dve.wait_ge(tile_in, 32 * (i + 1))
                dve.wait_ge(tile_attT_ready, i + 1)
                nc.vector.tensor_copy(tile_attT[:, :], sc[:, 0, 0:P]).then_inc(tile_attT_made, 1)
                then(nc.vector.tensor_tensor(tile_z[:, :], tile_x[:, :], bo_sb[:, :], ALU.add))
            elif wi == 1:
                dve.wait_ge(tile_y, i + 1)
                then(nc.vector.tensor_tensor(tile_z[:, :], tile_z[:, :], sc[:, 1, 0:E], ALU.add))
                layer_norm(then, tile_z[:, :], tile_x1[:, :], 1, t_norm, dve).then_inc(tile_x1_made, 1)
            elif wi == 2:
                dve.wait_ge(tile_x1T_ready, i + 1)
                nc.vector.tensor_copy(tile_x1T[:, :], sc[:, 0, 0:P]).then_inc(tile_x1T_made, 1)
            elif wi == 3:
                dve.wait_ge(tile_logits, i + 1)
                then(nc.vector.tensor_tensor(t_lg, sc[:, 1, 0:NR].rearrange("p (t r) -> p t r", r=NR), over_tiles(rb_sb, 1), ALU.add))
                then(nc.vector.tensor_reduce(t_four[0], t_lg, axis=AX.X, op=ALU.max))
                nc.vector.tensor_tensor(t_lg, t_lg, wide(t_four[0], 1), ALU.subtract).then_inc(tile_logits_made, 1)

        def copy_hidden(dve, i, k):
            dve.wait_ge(tile_hidden, 4 * i + k + 1)
            if k == 0:
                dve.wait_ge(tile_products, i + START)
            nc.vector.tensor_copy(tile_h[:, k * S:(k + 1) * S], sc[:, k % 2, :]).then_inc(tile_hidden_copied, 1)

        def tile_gates(dve, i, then):
            dve.wait_ge(tile_exp, i + 1)
            route(then, t_route, t_four, 1)
            then(nc.vector.scalar_tensor_tensor(tile_z[:, :], tile_x1[:, :], t_route[6][:, 0, NE:NE + 1], tile_x1[:, :], ALU.mult, ALU.add))

        def tile_finish(dve, i, then):
            dve.wait_ge(tile_products, i + 1 + START)
            for e in range(NE - 1):
                then(nc.vector.scalar_tensor_tensor(tile_z[:, :], sc[:, 1, e * P:(e + 1) * P], t_route[6][:, 0, e:e + 1],
                                                    tile_z[:, :], ALU.mult, ALU.add))
            e = NE - 1
            nc.vector.scalar_tensor_tensor(tile_z[:, :], sc[:, 1, e * P:(e + 1) * P], t_route[6][:, 0, e:e + 1],
                                           tile_z[:, :], ALU.mult, ALU.add).then_inc(tile_added, 1)
            dve.wait_ge(tile_added, i + 1)
            dve.wait_ge(tile_out_free, i + START)
            layer_norm(then, tile_z[:, :], tile_out[:, :], 1, t_norm, dve).then_inc(tile_done, 1)

        def vector_head(dve, n, nxt, i=None, part=0, then=None):
            if nxt is not None:
                mask_keys(dve, nxt)
                dve.wait_ge(probs_ready, NCH * n + START)
            for quad in range(4):
                for wi in range(4):
                    if nxt is not None:
                        if quad < 2:
                            copy_scores(dve, nxt, 4 * quad + wi)
                        elif quad == 2:
                            column_max(dve, nxt, wi)
                        elif wi == 0:
                            row_max(dve, nxt)
                        else:
                            for k in range(3 * (wi - 1), min(3 * wi, KT)):
                                subtract_max(dve, nxt, k)
                    if quad == 2 and part == 1:
                        tile_part_one_vector(dve, i, wi, then)
                    if wi % 2 == 1:
                        copy_numer(dve, n, quad, wi // 2)
                if quad == 2 and part == 1:
                    for k in range(4):
                        copy_hidden(dve, i, k)
                if quad == 2 and part == 2:
                    tile_finish(dve, i, then)
                normalise(dve, n, quad)
                if quad == 3 and part == 1:
                    tile_gates(dve, i, then)
            sum_wavelengths(dve, n)

        def vector_main(dve):
            mask_keys(dve, 0, first=True)
            for k in range(KT):
                copy_scores(dve, 0, k)
            for r in range(G):
                column_max(dve, 0, r)
            row_max(dve, 0)
            for k in range(KT):
                subtract_max(dve, 0, k)
            with dve.Fori(0, H) as n:
                vector_head(dve, n, n + 1)

            def pair(i, last):
                n = 2 * (i + FIRST_PAIR)
                counted = [0]
                then = stepper(dve, tile_step, TILE_STEPS * i, counted)
                vector_head(dve, n, n + 1, i, 1, then)
                vector_head(dve, n + 1, None if last else n + 2, i, 2, then)
                assert counted[0] == TILE_STEPS, counted
            with dve.Fori(0, PAIRS - FIRST_PAIR - 1) as i:
                pair(i, False)
            pair(PAIRS - FIRST_PAIR - 1, True)
        TILE_STEPS = 60

        gen_masked, gen_scores, gen_read = sem("gen_masked"), sem("gen_scores"), sem("gen_read")
        gen_step = sem("gen_step")
        gen_sine, gen_exp = sem("gen_sine"), sem("gen_exp")
        gen_angle, gen_shifted = sem("gen_angle"), sem("gen_shifted")
        gen_weighed = sem("gen_weighed")
        gen_tr, gen_tr_read, gen_pv = sem("gen_tr"), sem("gen_tr_read"), sem("gen_pv")
        g_raw, g_s, g_x, g_n, g_t, g_c = (scores[:, 0, i, :] for i in range(6))
        g_acc = scores[:, 0, 6, :]
        g_pT = scores[:, 0, 7, :]
        g_p = scores[:, 1, 0, :]
        g_max, g_neg, g_z, g_coef = (colmax[:, i:i + 1] for i in range(4))
        GEN_STEPS = 11

        def sync_general(sp):
            with sp.Fori(0, B) as b:
                sp.wait_ge(att_made, H * KT * b + START)
                load_qk(sp, b)
                load_v(sp, b)
                sp.wait_ge(att_made, H * KT * (b + 1) + START)
                store_att(sp, b)

        def tensor_general(pe):
            with pe.Fori(0, NH) as n:
                with pe.Fori(0, KT) as t:
                    j = n * KT + t
                    pe.wait_ge(gen_masked, j + 1)
                    for half in range(2):
                        cols = slice(half * HALF, (half + 1) * HALF)
                        last = nc.tensor.matmul(sc[:, 0, cols], km[:, 0:P], kt_[:, cols], start=True, stop=True)
                    last.then_inc(gen_scores, 1)
                    pe.wait_ge(gen_weighed, 2 * W * (j + 1))
                    for k in range(KT):
                        last = nc.tensor.transpose(sc[:, 1, k * P:(k + 1) * P], g_acc[:, k * P:(k + 1) * P], ident[:, :])
                    last.then_inc(gen_tr, 1)
                    pe.wait_ge(gen_tr_read, j + 1)
                    for k in range(KT):
                        last = nc.tensor.matmul(pv[:, 0, 0:D], g_pT[:, k * P:(k + 1) * P],
                                                vv[:, k, bass.ds((n % H) * D, D)], start=(k == 0), stop=(k == KT - 1))
                    last.then_inc(gen_pv, 1)

        def scalar_general(act):
            with act.Fori(0, NH * KT) as j:
                with act.Fori(0, W) as w:
                    act.wait_ge(gen_angle, j * W + w + 1)
                    nc.scalar.activation(g_c, g_t, ACT.Sin, scale=0.5).then_inc(gen_sine, 1)
                    act.wait_ge(gen_shifted, j * W + w + 1)
                    nc.scalar.activation(g_p, g_t, ACT.Exp, bias=g_neg, accum_out=g_z).then_inc(gen_exp, 1)

        def vector_general(dve):
            with dve.Fori(0, NH) as n:
                with dve.Fori(0, KT) as t:
                    j = n * KT + t
                    dve.wait_ge(qk_loaded, 32 * (n // H + 1))
                    dve.wait_ge(v_loaded, 16 * (n // H + 1))
                    dve.wait_ge(gen_scores, j + START)
                    nc.vector.tensor_scalar(km[:, 0:P], qt[:, bass.ds(t * P, P)], headmask[:, bass.ds(n % H, 1)], None,
                                            ALU.mult).then_inc(gen_masked, 1)
                    dve.wait_ge(gen_scores, j + 1 + START)
                    nc.vector.tensor_copy(g_raw, sc[:, 0, :])
                    dve.wait_ge(gen_tr, j + START)
                    nc.vector.memset(g_acc, 0.0).then_inc(gen_read, 1)
                    with dve.Fori(0, W) as w:
                        dve.wait_ge(gen_read, j + 1)
                        i = j * W + w
                        done = i * GEN_STEPS

                        nc.vector.tensor_scalar(g_s, g_raw, scales[:, bass.ds(w * H + n % H, 1)], None, ALU.mult).then_inc(gen_step, 1)
                        dve.wait_ge(gen_step, done + 1)
                        nc.vector.scalar_tensor_tensor(g_x, g_s, KERR, g_s, ALU.mult, ALU.mult).then_inc(gen_step, 1)
                        dve.wait_ge(gen_step, done + 2)
                        nc.vector.tensor_scalar(g_n, g_x, 1.0 / (2.0 * np.pi), MAGIC, ALU.mult, ALU.add).then_inc(gen_step, 1)
                        dve.wait_ge(gen_step, done + 3)
                        nc.vector.tensor_scalar(g_n, g_n, MAGIC, None, ALU.subtract).then_inc(gen_step, 1)
                        src = g_x
                        for part_no, part in enumerate(TWO_PI):
                            dve.wait_ge(gen_step, done + 4 + part_no)
                            nc.vector.scalar_tensor_tensor(g_t, g_n, -part, src, ALU.mult, ALU.add).then_inc(gen_step, 1)
                            src = g_t
                        dve.wait_ge(gen_step, done + 7)
                        nc.vector.tensor_scalar(g_t, g_t, PI, -PI, ALU.min, ALU.max).then_inc(gen_angle, 1)
                        dve.wait_ge(gen_sine, i + 1)
                        nc.vector.tensor_tensor(g_x, g_c, g_c, ALU.mult).then_inc(gen_step, 1)
                        dve.wait_ge(gen_step, done + 8)
                        nc.vector.tensor_scalar(g_x, g_x, -2.0, 1.0, ALU.mult, ALU.add).then_inc(gen_step, 1)
                        dve.wait_ge(gen_step, done + 9)
                        nc.vector.tensor_tensor(g_t, g_s, g_x, ALU.mult).then_inc(gen_step, 1)
                        dve.wait_ge(gen_step, done + 10)
                        nc.vector.tensor_reduce(g_neg, g_t, axis=AX.X, op=ALU.max, negate=True).then_inc(gen_shifted, 1)
                        dve.wait_ge(gen_exp, i + 1)
                        nc.vector.reciprocal(g_max, g_z).then_inc(gen_step, 1)
                        dve.wait_ge(gen_step, done + 11)
                        nc.vector.tensor_tensor(g_coef, g_max, wl_weight[:, bass.ds(w, 1)], ALU.mult).then_inc(gen_weighed, 1)
                        dve.wait_ge(gen_weighed, 2 * i + 1)
                        nc.vector.scalar_tensor_tensor(g_acc, g_p, g_coef, g_acc, ALU.mult, ALU.add).then_inc(gen_weighed, 1)
                        dve.wait_ge(gen_weighed, 2 * i + 2)
                        apart(dve)
                    dve.wait_ge(gen_tr, j + 1 + START)
                    nc.vector.tensor_copy(g_pT, sc[:, 1, :]).then_inc(gen_tr_read, 1)
                    dve.wait_ge(gen_pv, j + 1)
                    dve.wait_ge(att_stored, 32 * (n // H) + START)
                    nc.vector.tensor_copy(att[:, bass.ds((t % 2) * G + t // 2, 1), bass.ds((n % H) * D, D)].rearrange("p o d -> p (o d)"),
                                          pv[:, 0, 0:D]).then_inc(att_made, 1)

        weights = ring[:, :, :].rearrange("p s c -> p (s c)")
        w1_sb = weights[:, 0:NE * F].rearrange("p (e f) -> p e f", f=F)
        w2_sb = weights[:, NE * F:2 * NE * F].rearrange("p (e c d) -> p e c d", e=NE, d=E)
        pool_area = scores[:, :, :, :].rearrange("p a k s -> p (a k s)")

        def area(i, n=1):
            return pool_area[:, i * HALF:(i + n) * HALF]
        tiles = lambda a: a.rearrange("p (t e) -> p t e", e=E)
        xg, ag, aT, z, x1, x1T, z2, yo = (area(i) for i in range(8))
        hT = area(8, 2 * FC).rearrange("p (a c t) -> p a c t", a=2, t=HALF)
        g_norm = norm_views(area(16), GT)
        g_route = route_views(area(17), GT)
        lg, ex, gates = g_route[0], g_route[1], g_route[6]
        g_four = [area(18)[:, i * GT:(i + 1) * GT] for i in range(3)]

        ff_weights = sem("ff_weights")
        ff_in = sem("ff_in")
        ff_attT, ff_attT_made = sem("ff_attT"), sem("ff_attT_made")
        ff_y, ff_x1, ff_x1T, ff_x1T_made = sem("ff_y"), sem("ff_x1"), sem("ff_x1T"), sem("ff_x1T_made")
        ff_logits, ff_logits_made, ff_exp = sem("ff_logits"), sem("ff_logits_made"), sem("ff_exp")
        ff_hidden, ff_gelu = sem("ff_hidden"), sem("ff_gelu")
        ff_expert, ff_added = sem("ff_expert"), sem("ff_added")
        ff_step = sem("ff_step")
        ff_out, ff_stored = sem("ff_out"), sem("ff_stored")

        def sync_ff(sp, groups):
            first = NG - groups
            sp.wait_ge(att_stored, 32 * B + START)
            sp.dma_start(w1_sb.rearrange("p e f -> p (e f)"), w1.rearrange("d e f -> d (e f)")).then_inc(ff_weights, 16)
            sp.dma_start(w2_sb.rearrange("p e c d -> p (e c d)"), w2.rearrange("p e c d -> p (e c d)")).then_inc(ff_weights, 16)
            with sp.Fori(0, groups) as g:
                sp.wait_ge(ff_x1, g + START)
                sp.dma_start(tiles(xg), x_tiles[bass.ds((g + first) * GT, GT)].rearrange("t p e -> p t e")).then_inc(ff_in, 16)
                sp.dma_start(tiles(ag), att_dram[bass.ds((g + first) * GT, GT)].rearrange("t p e -> p t e")).then_inc(ff_in, 16)
                sp.wait_ge(ff_out, g + 1)
                sp.dma_start(out_tiles[bass.ds((g + first) * GT, GT)].rearrange("t p e -> p t e"), tiles(yo)).then_inc(ff_stored, 16)
            sp.wait_ge(ff_stored, 16 * groups + START)

        def hidden(pe, g, e):
            for c in range(FC):
                i = e * FC + c
                if i < 4:
                    pe.wait_ge(ff_gelu, NE * FC * g + START)
                else:
                    pe.wait_ge(ff_gelu, NE * FC * g + i - 3 + START)
                nc.tensor.matmul(sc[:, (i // 2) % 2, (i % 2) * HALF:(i % 2 + 1) * HALF], w1_sb[:, e, c * P:(c + 1) * P], x1T,
                                 start=True, stop=True).then_inc(ff_hidden, 1)

        def expert_out(pe, g, e):
            pe.wait_ge(ff_gelu, NE * FC * g + (e + 1) * FC + START)
            pe.wait_ge(ff_added, (NE * g + e - 1 if e >= 1 else NE * g) + START)
            for t in range(GT):
                for c in range(FC):
                    last = nc.tensor.matmul(tr[:, e % 2, t * P:(t + 1) * P], hT[:, e % 2, c, t * P:(t + 1) * P], w2_sb[:, e, c, :],
                                            start=(c == 0), stop=(c == FC - 1))
            last.then_inc(ff_expert, 1)

        def tensor_ff(pe, groups):
            pe.wait_ge(ff_weights, 32)
            with pe.Fori(0, groups) as g:
                pe.wait_ge(ff_in, 32 * (g + 1))
                for t in range(GT):
                    last = nc.tensor.transpose(pv[:, 0, t * P:(t + 1) * P], tiles(ag)[:, t, :], ident[:, :])
                last.then_inc(ff_attT, 1)
                pe.wait_ge(ff_attT_made, g + 1)
                for t in range(GT):
                    last = nc.tensor.matmul(pv[:, 1, t * P:(t + 1) * P], aT[:, t * P:(t + 1) * P], wo_sb[:, :], start=True, stop=True)
                last.then_inc(ff_y, 1)
                pe.wait_ge(ff_x1, g + 1 + START)
                for t in range(GT):
                    last = nc.tensor.transpose(pv[:, 0, t * P:(t + 1) * P], tiles(x1)[:, t, :], ident[:, :])
                last.then_inc(ff_x1T, 1)
                pe.wait_ge(ff_x1T_made, g + 1)
                for t in range(GT):
                    last = nc.tensor.matmul(pv[:, 1, t * NR:(t + 1) * NR], x1T[:, t * P:(t + 1) * P], rw_sb[:, :], start=True, stop=True)
                last.then_inc(ff_logits, 1)
                hidden(pe, g, 0)
                for e in range(NE):
                    if e + 1 < NE:
                        hidden(pe, g, e + 1)
                    expert_out(pe, g, e)

        def scalar_ff(act, groups):
            with act.Fori(0, groups) as g:
                act.wait_ge(ff_logits_made, g + 1)
                nc.scalar.activation(ex, lg, ACT.Exp).then_inc(ff_exp, 1)
                for i in range(NE * FC):
                    act.wait_ge(ff_hidden, NE * FC * g + i + 1)
                    if i // FC >= 2 and i % FC == 0:
                        act.wait_ge(ff_expert, NE * g + i // FC - 1 + START)
                    elif i % FC == 0:
                        act.wait_ge(ff_expert, NE * g + START)
                    nc.scalar.activation(hT[:, (i // FC) % 2, i % FC, :], sc[:, (i // 2) % 2, (i % 2) * HALF:(i % 2 + 1) * HALF],
                                         ACT.Gelu).then_inc(ff_gelu, 1)

        def vector_ff(dve, groups):
            def body(g, then):
                dve.wait_ge(ff_in, 32 * (g + 1))
                then(nc.vector.tensor_tensor(tiles(z), tiles(xg), over_tiles(bo_sb, GT), ALU.add))
                dve.wait_ge(ff_attT, g + 1)
                nc.vector.tensor_copy(aT, pv[:, 0, :]).then_inc(ff_attT_made, 1)
                dve.wait_ge(ff_y, g + 1)
                then(nc.vector.tensor_tensor(z, z, pv[:, 1, :], ALU.add))
                layer_norm(then, z, x1, GT, g_norm, dve).then_inc(ff_x1, 1)
                dve.wait_ge(ff_x1T, g + 1)
                nc.vector.tensor_copy(x1T, pv[:, 0, :]).then_inc(ff_x1T_made, 1)
                dve.wait_ge(ff_logits, g + 1)
                then(nc.vector.tensor_tensor(lg, pv[:, 1, 0:GT * NR].rearrange("p (t r) -> p t r", r=NR), over_tiles(rb_sb, GT), ALU.add))
                then(nc.vector.tensor_reduce(g_four[0], lg, axis=AX.X, op=ALU.max))
                nc.vector.tensor_tensor(lg, lg, wide(g_four[0], GT), ALU.subtract).then_inc(ff_logits_made, 1)
                dve.wait_ge(ff_exp, g + 1)
                route(then, g_route, g_four, GT)
                for t in range(GT):
                    last = nc.vector.scalar_tensor_tensor(tiles(z2)[:, t, :], tiles(x1)[:, t, :], gates[:, t, NE:NE + 1],
                                                          tiles(x1)[:, t, :], ALU.mult, ALU.add)
                then(last)
                for e in range(NE):
                    dve.wait_ge(ff_expert, NE * g + e + 1 + START)
                    if e:
                        dve.wait_ge(ff_added, NE * g + e + START)
                    for t in range(GT):
                        last = nc.vector.scalar_tensor_tensor(tiles(z2)[:, t, :], tr[:, e % 2, t * P:(t + 1) * P], gates[:, t, e:e + 1],
                                                              tiles(z2)[:, t, :], ALU.mult, ALU.add)
                    last.then_inc(ff_added, 1)
                dve.wait_ge(ff_added, NE * (g + 1) + START)
                dve.wait_ge(ff_stored, 16 * g + START)
                layer_norm(then, z2, yo, GT, g_norm, dve).then_inc(ff_out, 1)

            with dve.Fori(0, groups) as g:
                counted = [0]
                body(g, stepper(dve, ff_step, FF_STEPS * g, counted))
                assert counted[0] == FF_STEPS, counted
        FF_STEPS = 53

        @block.sync
        def _(sp):
            sync_setup(sp)
            sp.wait_ge(qkv_stored, 48 * B + START)
            sp.wait_ge(flag_ready, 1)
            safe = sp.value_load(flag[0:1, 0:1], min_val=0, max_val=1)
            with sp.If(safe == 1):
                sync_main(sp)
                sync_ff(sp, TAIL)
            with sp.Else():
                sync_general(sp)
                sync_ff(sp, NG)

        @block.gpsimd
        def _(pool):
            pool_setup(pool)
            pool.wait_ge(flag_ready, 1)
            safe = pool.value_load(flag[0:1, 0:1], min_val=0, max_val=1)
            with pool.If(safe == 1):
                pool_main(pool)
            with pool.Else():
                pool.nop()

        @block.scalar
        def _(act):
            scalar_setup(act)
            act.wait_ge(flag_ready, 1)
            safe = act.value_load(flag[0:1, 0:1], min_val=0, max_val=1)
            with act.If(safe == 1):
                scalar_main(act)
                scalar_ff(act, TAIL)
            with act.Else():
                scalar_general(act)
                scalar_ff(act, NG)

        @block.tensor
        def _(pe):
            tensor_setup(pe)
            pe.wait_ge(flag_ready, 1)
            safe = pe.value_load(flag[0:1, 0:1], min_val=0, max_val=1)
            with pe.If(safe == 1):
                tensor_main(pe)
                tensor_ff(pe, TAIL)
            with pe.Else():
                tensor_general(pe)
                tensor_ff(pe, NG)

        @block.vector
        def _(dve):
            vector_setup(dve)
            dve.wait_ge(flag_ready, 1)
            safe = dve.value_load(flag[0:1, 0:1], min_val=0, max_val=1)
            with dve.If(safe == 1):
                vector_main(dve)
                vector_ff(dve, TAIL)
            with dve.Else():
                vector_general(dve)
                vector_ff(dve, NG)


_INS = ["L0_attn_x", "L0_attn_Wq", "L0_attn_bq", "L0_attn_Wk", "L0_attn_bk", "L0_attn_Wv", "L0_attn_bv",
        "L0_attn_Wo", "L0_attn_bo", "L0_attn_phase_modulators", "L0_attn_interference_weights",
        "L0_ffn_router_w", "L0_ffn_router_b", "L0_ffn_w1", "L0_ffn_w2"]


def lay_out(name, a):
    a = np.asarray(a)
    if name == "L0_ffn_w1":
        a = a.transpose(1, 0, 2)
    elif name == "L0_ffn_w2":
        a = a.reshape(NE, FC, P, E).transpose(2, 0, 1, 3)
    return np.ascontiguousarray(a)


def kernel(**inputs):
    import concourse.bacc as bacc
    from concourse.bass_utils import run_bass_kernel_spmd

    nc = bacc.Bacc("TRN2", target_bir_lowering=False, num_devices=1)
    arrays, args = {}, []
    for name in _INS:
        a = lay_out(name, inputs[name])
        arrays[f"in_{name}"] = a
        args.append(nc.dram_tensor(f"in_{name}", a.shape, mybir.dt.from_np(a.dtype), kind="ExternalInput").ap())
    args.append(nc.dram_tensor("out", (B, S, E), FP32, kind="ExternalOutput").ap())
    build(nc, *args)
    r = run_bass_kernel_spmd(nc, [arrays], core_ids=[0])
    return r.results[0]["out"]
```

```python
from contextlib import ExitStack

import numpy as np
import concourse.bass as bass
from concourse import mybir

FP32 = mybir.dt.float32
I32 = mybir.dt.int32
ALU = mybir.AluOpType
ACT = mybir.ActivationFunctionType
AX = mybir.AxisListType

P = 128
B, S, E = 4, 1024, 128
H, D, W = 16, 8, 16
NE, F, NR = 8, 512, 9
KT = S // P
HALF = 512
NH = B * H
VC = 32
G = 4
QG = S // G
NCH = 2 * W
CK = KT // 2
SLOTS = 4
GT = 4
NG = B * S // (GT * P)
FC = F // P
TAIL = KT // GT
PAIRS = NH // 2
FIRST_PAIR = H // 2
SCALE = 1.0 / np.sqrt(D)
KERR = 2.7e-18 * 1000000.0
EPS = 1e-5
SAFE_SCORE = 9000.0
SAFE_PRODUCT = SAFE_SCORE / (SCALE * D)
MAGIC = 1.5 * 2.0 ** 23
TWO_PI = (6.28125, 0.0019352436065673828, 6.357301884918343e-08)
PI = 3.1415925
RSQRT_SEED = float(0x5F3759DF)
LOG2E = float(np.log2(np.e))
EXP2 = (0.6931469775987168, 0.24022242084634685, 0.05550733743574262, 0.009671512688178108, 0.0013264727247206184)
EXP2_LOW = -127.0
VSTEPS = 10
START = 1
SP_FULLS, SP_FREES = KT + 2, KT + 1


def build(nc, x, wq, bq, wk, bk, wv, bv, wo, bo, pm, iw, rw, rb, w1, w2, out):
    qt_dram = nc.dram_tensor("qt_scratch", (B, P, S), FP32, kind="Internal").ap()
    kt_dram = nc.dram_tensor("kt_scratch", (B, P, S), FP32, kind="Internal").ap()
    v_dram = nc.dram_tensor("v_scratch", (B, P, KT, E), FP32, kind="Internal").ap()
    att_dram = nc.dram_tensor("att_scratch", (B * S // P, P, E), FP32, kind="Internal").ap()
    x_tiles = x.rearrange("b (t p) e -> (b t) p e", p=P)
    out_tiles = out.rearrange("b (t p) e -> (b t) p e", p=P)

    ctx = ExitStack()
    with ctx:
        def sb(name, shape, dt=FP32):
            return ctx.enter_context(nc.sbuf_tensor(name, shape, dt))

        def ps(name, shape):
            return ctx.enter_context(nc.psum_tensor(name, shape, FP32))

        def sem(name):
            return ctx.enter_context(nc.semaphore(name))

        ident = sb("ident", [P, P])
        headmask = sb("headmask", [P, H])
        rank = sb("rank", [P, NR])
        scales = sb("scales", [P, W * H])
        pm_sb = sb("pm_sb", [P, W * H])
        scales_log2 = sb("scales_log2", [P, W * H])
        wl_weight = sb("wl_weight", [P, W])
        wl_wide = sb("wl_wide", [P, W // 2, 8, 2])
        wo_sb = sb("wo_sb", [P, E])
        bq_sb, bk_sb = sb("bq_sb", [P, 1]), sb("bk_sb", [P, 1])
        bo_sb = sb("bo_sb", [P, E])
        rw_sb, rb_sb = sb("rw_sb", [P, NR]), sb("rb_sb", [P, NR])
        peak = sb("peak", [P, 2 * B])
        peak_row = sb("peak_row", [1, 2])
        product = sb("product", [1, 1])
        flag = sb("flag", [1, 1], I32)

        qt = sb("qt", [P, S])
        kt_ = sb("kt_", [P, S])
        vv = sb("vv", [P, KT, E])
        km = sb("km", [P, S])
        scores = sb("scores", [P, 2, KT, S])
        ring = sb("ring", [P, SLOTS, CK * S])
        vh = sb("vh", [P, 2, KT, VC])
        colmax = km
        vprobs = sb("vprobs", [P, 2, HALF])
        vpower = sb("vpower", [P, HALF])
        vrest = sb("vrest", [P, HALF])
        rowmax = sb("rowmax", [P, KT])
        numer = sb("numer", [P, 2, HALF])
        recip = sb("recip", [P, 32])
        coef = sb("coef", [P, 32])
        parts = sb("parts", [P, W // 2, 8, 2, D])
        att = sb("att", [P, KT, E])

        tile_w = sb("tile_w", [P, NE * F])
        tile_h = sb("tile_h", [P, NE * F])
        tile_x, tile_att, tile_attT, tile_z, tile_x1, tile_x1T, tile_out = (
            sb(n, [P, E]) for n in ("tile_x", "tile_att", "tile_attT", "tile_z", "tile_x1", "tile_x1T", "tile_out"))
        tile_small = sb("tile_small", [P, 96])

        pv = ps("pv", [P, 2, HALF])
        tr = ps("tr", [P, 2, HALF])
        sc = ps("sc", [P, 2, S])

        consts_loaded = sem("consts_loaded")
        consts_made = sem("consts_made")
        mask_zeroed = sem("mask_zeroed")
        flag_ready = sem("flag_ready")

        block = ctx.enter_context(nc.Block())

        def apart(engine):
            engine.nop(nofuse=True)

        scale_step = sem("scale_step")
        sine_ready = sem("sine_ready")
        x_loaded = sem("x_loaded")
        xT_ready, xT_made = sem("xT_ready"), sem("xT_made")
        q_mm, k_mm, v_mm = sem("q_mm"), sem("k_mm"), sem("v_mm")
        q_made, k_made, v_made = sem("q_made"), sem("k_made"), sem("v_made")
        peak_made = sem("peak_made")
        qkv_stored = sem("qkv_stored")
        peak_rows, peak_step = sem("peak_rows"), sem("peak_step")
        xa = scores[:, 0, 0, :].rearrange("p (t e) -> p t e", e=E)
        xT = scores[:, 0, 1, :]
        wq_sb, wk_sb, wv_sb, bv_sb = (scores[:, 0, 2, i * E:(i + 1) * E] for i in range(4))
        trig = scales_log2
        CONST_DMAS = 12

        def sync_setup(sp):
            def everywhere(ap, n):
                return ap.rearrange("(o n) -> o n", o=1).to_broadcast([P, n])
            loads = [(wq_sb[:, :], wq), (wk_sb[:, :], wk), (wv_sb[:, :], wv), (wo_sb[:, :], wo),
                     (bq_sb[:, :], bq.rearrange("(p o) -> p o", o=1)),
                     (bk_sb[:, :], bk.rearrange("(p o) -> p o", o=1)),
                     (bv_sb[:, :], everywhere(bv, E)), (bo_sb[:, :], everywhere(bo, E)),
                     (rw_sb[:, :], rw), (rb_sb[:, :], everywhere(rb, NR)),
                     (pm_sb[:, :], everywhere(pm.rearrange("w h -> (w h)"), W * H)),
                     (wl_weight[:, :], everywhere(iw, W))]
            for dst, src in loads:
                sp.dma_start(dst, src).then_inc(consts_loaded, 16)
            with sp.Fori(0, B) as b:
                sp.wait_ge(xT_ready, b + START)
                sp.dma_start(xa, x_tiles[bass.ds(b * KT, KT)].rearrange("t p e -> p t e")).then_inc(x_loaded, 16)
                sp.wait_ge(q_made, b + 1 + START)
                sp.dma_start(qt_dram[bass.ds(b, 1)].rearrange("o p s -> p (o s)"), qt[:, :]).then_inc(qkv_stored, 16)
                sp.wait_ge(k_made, b + 1 + START)
                sp.dma_start(kt_dram[bass.ds(b, 1)].rearrange("o p s -> p (o s)"), kt_[:, :]).then_inc(qkv_stored, 16)
                sp.wait_ge(v_made, b + 1 + START)
                sp.dma_start(v_dram[bass.ds(b, 1)].rearrange("o p t e -> p (o t) e"), vv[:, :, :]).then_inc(qkv_stored, 16)

        def pool_setup(pool):
            for started in (xT_ready, q_made, k_made, v_mm, v_made, peak_made, qkv_stored, probs_ready, tr_full,
                            tr_read, att_made, att_stored, gen_scores, gen_tr, ff_x1, ff_gelu, ff_expert,
                            ff_added, ff_stored, tile_x1_made, tile_products, tile_out_free):
                pool.sem_inc(started, START)
            nc.gpsimd.memset(ident[:, :], 1.0)
            nc.gpsimd.memset(headmask[:, :], 1.0)
            for e in range(NR):
                nc.gpsimd.memset(rank[:, e:e + 1], float(NR - e))
            nc.gpsimd.memset(vh[:, :, :, :], 0.0).then_inc(mask_zeroed, 1)
            pool.wait_ge(mask_zeroed, 1)
            nc.gpsimd.memset(vh[:, :, :, D:D + 1], 1.0)
            nc.gpsimd.affine_select(out=ident[:, :], in_=ident[:, :], compare_op=ALU.is_equal, fill=0.0,
                                    base=0, pattern=[[-1, P]], channel_multiplier=1)
            nc.gpsimd.affine_select(out=headmask[:, :], in_=headmask[:, :], compare_op=ALU.is_ge, fill=0.0,
                                    base=0, pattern=[[-D, H]], channel_multiplier=1).then_inc(mask_zeroed, 1)
            pool.wait_ge(mask_zeroed, 2)
            nc.gpsimd.affine_select(out=headmask[:, :], in_=headmask[:, :], compare_op=ALU.is_ge, fill=0.0,
                                    base=D - 1, pattern=[[D, H]], channel_multiplier=-1).then_inc(consts_made, 1)

        def scalar_setup(act):
            act.wait_ge(scale_step, 5)
            nc.scalar.activation(trig[:, :], trig[:, :], ACT.Sin, scale=0.5).then_inc(sine_ready, 1)
            act.wait_ge(consts_loaded, 16 * CONST_DMAS)
            act.preload_act_table(ACT.Exp)
            with act.Fori(0, B) as b:
                act.wait_ge(q_mm, b + 1)
                act.wait_ge(qkv_stored, 48 * b + START)
                act.wait_ge(peak_made, b + START)
                nc.scalar.activation(qt[:, :], sc[:, 1, :], ACT.Identity, bias=bq_sb[:, 0:1]).then_inc(q_made, 1)
                act.wait_ge(k_mm, b + 1)
                nc.scalar.activation(kt_[:, :], sc[:, 0, :], ACT.Identity, bias=bk_sb[:, 0:1]).then_inc(k_made, 1)

        def tensor_setup(pe):
            pe.wait_ge(consts_made, 1)
            pe.wait_ge(consts_loaded, 16 * CONST_DMAS)
            with pe.Fori(0, B) as b:
                pe.wait_ge(x_loaded, 16 * (b + 1))
                pe.wait_ge(k_made, b + START)
                for t in range(KT):
                    last = nc.tensor.transpose(sc[:, 0, t * P:(t + 1) * P], xa[:, t, :], ident[:, :])
                last.then_inc(xT_ready, 1)
                pe.wait_ge(xT_made, b + 1)
                pe.wait_ge(q_made, b + START)
                for half in range(2):
                    cols = slice(half * HALF, (half + 1) * HALF)
                    last = nc.tensor.matmul(sc[:, 1, cols], wq_sb[:, :], xT[:, cols], start=True, stop=True)
                last.then_inc(q_mm, 1)
                for half in range(2):
                    cols = slice(half * HALF, (half + 1) * HALF)
                    last = nc.tensor.matmul(sc[:, 0, cols], wk_sb[:, :], xT[:, cols], start=True, stop=True)
                last.then_inc(k_mm, 1)
                pe.wait_ge(v_made, b + START)
                for t in range(KT):
                    last = nc.tensor.matmul(tr[:, t // 4, (t % 4) * P:(t % 4 + 1) * P], xT[:, t * P:(t + 1) * P],
                                            wv_sb[:, :], start=True, stop=True)
                last.then_inc(v_mm, 1)
            pe.wait_ge(peak_step, 1)
            for i in range(2):
                last = nc.tensor.matmul(pv[0:1, 0, i * P:(i + 1) * P], peak[:, i:i + 1], ident[:, :],
                                        start=True, stop=True)
            last.then_inc(peak_rows, 1)

        def vector_setup(dve):
            dve.wait_ge(consts_loaded, 16 * CONST_DMAS)
            whole = colmax[:, 0:W * H]
            nc.vector.tensor_scalar(wl_wide[:, :, :, :], wl_weight[:, :].rearrange("p (a o w) -> p a o w", o=1, w=2).to_broadcast([P, W // 2, 8, 2]),
                                    1.0 / W, None, ALU.mult)
            nc.vector.tensor_scalar(whole, pm_sb[:, :], 1.0 / (2.0 * np.pi), MAGIC, ALU.mult, ALU.add).then_inc(scale_step, 1)
            dve.wait_ge(scale_step, 1)
            nc.vector.tensor_scalar(whole, whole, MAGIC, None, ALU.subtract).then_inc(scale_step, 1)
            src = pm_sb[:, :]
            for i, part in enumerate(TWO_PI):
                dve.wait_ge(scale_step, 2 + i)
                nc.vector.scalar_tensor_tensor(trig[:, :], whole, -part, src, ALU.mult, ALU.add).then_inc(scale_step, 1)
                src = trig[:, :]
            dve.wait_ge(sine_ready, 1)
            nc.vector.tensor_tensor(pm_sb[:, :], trig[:, :], trig[:, :], ALU.mult).then_inc(scale_step, 1)
            dve.wait_ge(scale_step, 6)
            nc.vector.tensor_scalar(trig[:, :], pm_sb[:, :], -2.0, 1.0, ALU.mult, ALU.add).then_inc(scale_step, 1)
            dve.wait_ge(scale_step, 7)
            nc.vector.tensor_tensor(pm_sb[:, :], trig[:, :], trig[:, :], ALU.mult).then_inc(scale_step, 1)
            dve.wait_ge(scale_step, 8)
            nc.vector.tensor_scalar(scales[:, :], pm_sb[:, :], SCALE, None, ALU.mult).then_inc(scale_step, 1)
            nc.vector.tensor_scalar(scales_log2[:, :], pm_sb[:, :], SCALE * LOG2E, None, ALU.mult).then_inc(scale_step, 1)
            dve.wait_ge(scale_step, 10)
            nc.vector.tensor_scalar(wl_weight[:, :], wl_weight[:, :], 1.0 / W, None, ALU.mult)
            with dve.Fori(0, B) as b:
                dve.wait_ge(xT_ready, b + 1 + START)
                dve.wait_ge(v_mm, b + START)
                nc.vector.tensor_copy(xT, sc[:, 0, :]).then_inc(xT_made, 1)
                dve.wait_ge(v_mm, b + 1 + START)
                dve.wait_ge(qkv_stored, 48 * b + START)
                nc.vector.tensor_tensor(vv[:, :, :], tr[:, :, :].rearrange("p a (t e) -> p (a t) e", e=E),
                                        bv_sb[:, :].rearrange("p (o e) -> p o e", o=1).to_broadcast([P, KT, E]),
                                        ALU.add).then_inc(v_made, 1)
                dve.wait_ge(q_made, b + 1 + START)
                nc.vector.tensor_reduce(peak[:, bass.ds(b, 1)], qt[:, :], axis=AX.X, op=ALU.max,
                                        apply_absolute_value=True)
                dve.wait_ge(k_made, b + 1 + START)
                nc.vector.tensor_reduce(peak[:, bass.ds(b + B, 1)], kt_[:, :], axis=AX.X, op=ALU.max,
                                        apply_absolute_value=True).then_inc(peak_made, 1)
            dve.wait_ge(peak_made, B + START)
            nc.vector.tensor_reduce(recip[:, 0:2], peak[:, :].rearrange("p (i b) -> p i b", b=B), axis=AX.X, op=ALU.max).then_inc(peak_made, 1)
            dve.wait_ge(peak_made, B + 1 + START)
            nc.vector.tensor_copy(peak[:, 0:2], recip[:, 0:2]).then_inc(peak_step, 1)
            dve.wait_ge(peak_rows, 1)
            nc.vector.tensor_reduce(peak_row[:, :], pv[0:1, 0, 0:2 * P].rearrange("p (i q) -> p i q", q=P), axis=AX.X,
                                    op=ALU.max).then_inc(peak_step, 1)
            dve.wait_ge(peak_step, 2)
            nc.vector.tensor_tensor(product[:, :], peak_row[:, 0:1], peak_row[:, 1:2], ALU.mult).then_inc(peak_step, 1)
            dve.wait_ge(peak_step, 3)
            nc.vector.tensor_scalar(flag[:, :], product[:, :], SAFE_PRODUCT, None, ALU.is_lt).then_inc(flag_ready, 1)

        def stepper(dve, signal, base, counted):
            def then(ins):
                ins.then_inc(signal, 1)
                counted[0] += 1
                dve.wait_ge(signal, base + counted[0])
            return then

        def over_tiles(row, nt):
            n = row.shape[1]
            return row[:, :].rearrange("p (o n) -> p o n", o=1).to_broadcast([P, nt, n])

        def wide(a, nt):
            return a.rearrange("p (t o) -> p t o", o=1).to_broadcast([P, nt, NR])

        def norm_views(a, nt):
            cols = [a[:, i * nt:(i + 1) * nt] for i in range(8, 11)]
            return (a[:, 0:6 * nt].rearrange("p (t s) -> p t s", s=6), a[:, 6 * nt:8 * nt].rearrange("p (t s) -> p t s", s=2), *cols)

        def route_views(a, nt):
            return [a[:, i * NR * nt:(i + 1) * NR * nt].rearrange("p (t r) -> p t r", r=NR) for i in range(7)]

        def layer_norm(then, src, dst, nt, views, dve):
            stats, mv, var_, y_, t_ = views
            src, dst = (a.rearrange("p (t e) -> p t e", e=E) for a in (src, dst))
            for t in range(nt):
                last = nc.vector.bn_stats(stats[:, t, :], src[:, t, :])
            then(last)
            apart(dve)
            for t in range(nt):
                last = nc.vector.bn_aggr(mv[:, t, :], stats[:, t, :])
            then(last)
            then(nc.vector.tensor_scalar(var_, mv[:, :, 1], EPS, None, ALU.add))
            then(nc.vector.tensor_scalar(y_.bitcast(I32), var_.bitcast(I32), -0.5, RSQRT_SEED, ALU.mult, ALU.add))
            for _ in range(4):
                then(nc.vector.tensor_tensor(t_, y_, y_, ALU.mult))
                then(nc.vector.scalar_tensor_tensor(t_, t_, -0.5, var_, ALU.mult, ALU.mult))
                then(nc.vector.scalar_tensor_tensor(y_, t_, 1.5, y_, ALU.add, ALU.mult))
            for t in range(nt):
                last = nc.vector.tensor_scalar(dst[:, t, :], src[:, t, :], mv[:, t, 0:1], y_[:, t:t + 1], ALU.subtract, ALU.mult)
            return last

        def route(then, views, four, nt):
            lg, ex, pr, eq, oh, oh2, gates = views
            m4, s4, r4 = four

            def pick(dst, src):
                then(nc.vector.tensor_reduce(m4, src, axis=AX.X, op=ALU.max))
                then(nc.vector.tensor_tensor(eq, src, wide(m4, nt), ALU.is_equal))
                then(nc.vector.tensor_tensor(eq, eq, over_tiles(rank, nt), ALU.mult))
                then(nc.vector.tensor_reduce(m4, eq, axis=AX.X, op=ALU.max))
                then(nc.vector.tensor_tensor(dst, eq, wide(m4, nt), ALU.is_equal))

            then(nc.vector.tensor_reduce(s4, ex, axis=AX.X, op=ALU.add))
            then(nc.vector.reciprocal(r4, s4))
            then(nc.vector.tensor_tensor(pr, ex, wide(r4, nt), ALU.mult))
            pick(oh, pr)
            then(nc.vector.scalar_tensor_tensor(lg, oh, -2.0, pr, ALU.mult, ALU.add))
            pick(oh2, lg)
            then(nc.vector.tensor_tensor(oh, oh, oh2, ALU.add))
            then(nc.vector.tensor_tensor(gates, oh, pr, ALU.mult))

        t_norm = norm_views(tile_small, 1)
        t_route = route_views(tile_small[:, 11:11 + 7 * NR], 1)
        t_lg, t_ex = t_route[0], t_route[1]
        t_four = [tile_small[:, i:i + 1] for i in range(74, 77)]

        qk_loaded, v_loaded = sem("qk_loaded"), sem("v_loaded")
        att_made, att_stored = sem("att_made"), sem("att_stored")

        def load_qk(sp, b):
            sp.dma_start(qt[:, :], qt_dram[bass.ds(b, 1)].rearrange("o p s -> p (o s)")).then_inc(qk_loaded, 16)
            sp.dma_start(kt_[:, :], kt_dram[bass.ds(b, 1)].rearrange("o p s -> p (o s)")).then_inc(qk_loaded, 16)

        def load_v(sp, b):
            sp.dma_start(vv[:, :, :], v_dram[bass.ds(b, 1)].rearrange("o p t e -> p (o t) e")).then_inc(v_loaded, 16)

        def store_att(sp, b):
            for qh in range(2):
                sp.dma_start(att_dram[bass.ds(b * KT + 4 * qh, 4)].rearrange("q p e -> p q e"),
                             att[:, :, :].rearrange("p (qb qh) e -> p qh qb e", qh=2)[:, qh]).then_inc(att_stored, 16)

        km_ready = sem("km_ready")
        sc_full = sem("sc_full")
        sc_free = sem("sc_free")
        colmax_ready = sem("colmax_ready")
        diff_ready = sem("diff_ready")
        probs_ready = sem("probs_ready")
        vexp_step = sem("vexp_step")
        slot_free = sem("slot_free")
        vh_ready = sem("vh_ready")
        pv_read = sem("pv_read")
        tr_full, tr_read = sem("tr_full"), sem("tr_read")
        norm_step = sem("norm_step")
        tile_in, tile_w1, tile_w2 = sem("tile_in"), sem("tile_w1"), sem("tile_w2")
        tile_attT_ready, tile_attT_made, tile_y = sem("tile_attT_ready"), sem("tile_attT_made"), sem("tile_y")
        tile_x1_made, tile_x1T_ready, tile_x1T_made = sem("tile_x1_made"), sem("tile_x1T_ready"), sem("tile_x1T_made")
        tile_logits, tile_logits_made, tile_exp = sem("tile_logits"), sem("tile_logits_made"), sem("tile_exp")
        tile_hidden, tile_hidden_copied = sem("tile_hidden"), sem("tile_hidden_copied")
        tile_gelu, tile_products, tile_added = sem("tile_gelu"), sem("tile_products"), sem("tile_added")
        tile_step, tile_done, tile_stored, tile_out_free = (
            sem("tile_step"), sem("tile_done"), sem("tile_stored"), sem("tile_out_free"))

        def sync_main(sp):
            load_qk(sp, 0)
            load_v(sp, 0)
            with sp.Fori(1, B) as b:
                sp.wait_ge(sc_full, SP_FULLS * H * b)
                load_qk(sp, b)
                sp.wait_ge(vh_ready, H * b)
                load_v(sp, b)
                sp.wait_ge(att_made, H * b + START)
                store_att(sp, b - 1)
                sp.wait_ge(att_stored, 32 * b + START)
                apart(sp)
                with sp.Fori(0, KT) as t:
                    i = (b - 1) * KT + t
                    sp.wait_ge(tile_x1_made, i + START)
                    sp.dma_start(tile_x[:, :], x_tiles[bass.ds(i, 1)].rearrange("o p e -> p (o e)")).then_inc(tile_in, 16)
                    sp.dma_start(tile_att[:, :], att_dram[bass.ds(i, 1)].rearrange("o p e -> p (o e)")).then_inc(tile_in, 16)
                    sp.wait_ge(tile_products, i + START)
                    sp.dma_start(tile_w[:, :], w1.rearrange("d e f -> d (e f)")).then_inc(tile_w1, 16)
                    sp.wait_ge(tile_hidden, 4 * (i + 1))
                    sp.dma_start(tile_w[:, :], w2.rearrange("p e c d -> p (e c d)")).then_inc(tile_w2, 16)
            sp.wait_ge(att_made, H * B + START)
            store_att(sp, B - 1)

        def copy_values(pool, n, buf):
            pool.wait_ge(v_loaded, 16 * (n // H + 1))
            pool.wait_ge(slot_free, NCH * (n - 1) + SLOTS)
            nc.gpsimd.tensor_copy(vh[:, buf, :, 0:D], vv[:, :, bass.ds((n % H) * D, D)]).then_inc(vh_ready, 1)

        def pool_main(pool):
            pool.sem_inc(slot_free, SLOTS)
            pool.wait_ge(v_loaded, 16)
            nc.gpsimd.tensor_copy(vh[:, 0, :, 0:D], vv[:, :, 0:D]).then_inc(vh_ready, 1)
            nc.gpsimd.tensor_copy(vh[:, 1, :, 0:D], vv[:, :, D:2 * D]).then_inc(vh_ready, 1)
            with pool.Fori(1, FIRST_PAIR) as i:
                copy_values(pool, 2 * i, 0)
                copy_values(pool, 2 * i + 1, 1)
            with pool.Fori(0, PAIRS - FIRST_PAIR) as i:
                copy_values(pool, 2 * (i + FIRST_PAIR), 0)
                copy_values(pool, 2 * (i + FIRST_PAIR) + 1, 1)
                pool.wait_ge(tile_done, i + 1)
                pool.dma_start(out_tiles[bass.ds(i, 1)].rearrange("o p e -> p (o e)"), tile_out[:, :]).then_inc(tile_stored, 16)
                pool.wait_ge(tile_stored, 16 * (i + 1))
                pool.sem_inc(tile_out_free, 1)

        def scalar_main(act):
            act.preload_act_table(ACT.Exp)
            scale_bits = scales[0:1, :].bitcast(I32)
            scale = [act.alloc_register(f"scale_{w2}") for w2 in range(2)]

            def quads(n, first, last):
                with act.Fori(first, last) as quad:
                    for i in range(8):
                        pair, half, w2 = i // 4, (i // 2) % 2, i % 2
                        w, chunk = 4 * quad + 2 * pair + w2, NCH * n + 8 * quad + i
                        if i in (0, 2):
                            act.wait_ge(diff_ready, KT * n + CK * (half + 1))
                        if half == 0:
                            act.reg_load(scale[w2], scale_bits[:, bass.ds(w * H + n % H, 1)])
                        act.wait_ge(slot_free, chunk + 1)
                        apart(act)
                        cols = CK * S - (HALF if half == 1 and w2 == 1 else 0)
                        nc.scalar.activation(ring[:, i % SLOTS, 0:cols],
                                             scores[:, bass.ds(n % 2, 1), half * CK:(half + 1) * CK, :].rearrange("p o k s -> p (o k s)")[:, 0:cols],
                                             ACT.Exp, scale=scale[w2]).then_inc(probs_ready, 1)

            with act.Fori(0, H) as n:
                quads(n, 0, 4)
            with act.Fori(0, PAIRS - FIRST_PAIR) as i:
                n = 2 * (i + FIRST_PAIR)
                quads(n, 0, 3)
                act.wait_ge(tile_logits_made, i + 1)
                nc.scalar.activation(t_ex, t_lg, ACT.Exp).then_inc(tile_exp, 1)
                quads(n, 3, 4)
                quads(n + 1, 0, 1)
                act.wait_ge(tile_hidden_copied, 4 * (i + 1))
                nc.scalar.activation(tile_h[:, :], tile_h[:, :], ACT.Gelu).then_inc(tile_gelu, 1)
                act.preload_act_table(ACT.Exp)
                quads(n + 1, 1, 4)

        def score_tile(pe, m, k, first=False):
            if k == 0:
                pe.wait_ge(km_ready, m + 1)
                if not first:
                    pe.wait_ge(sc_free, SP_FREES * m)
            elif k == 1:
                if not first:
                    pe.wait_ge(diff_ready, KT * m)
            else:
                pe.wait_ge(sc_free, SP_FREES * m + k - 1)
            for half in range(2):
                cols = slice(half * HALF, (half + 1) * HALF)
                last = nc.tensor.matmul(sc[:, k % 2, cols], km[:, k * P:(k + 1) * P], qt[:, cols], start=True, stop=True)
            last.then_inc(sc_full, 1)

        def transpose_colmax(pe, m, tile_no=None):
            pe.wait_ge(colmax_ready, m + 1)
            if tile_no is not None:
                pe.wait_ge(tile_hidden_copied, 4 * tile_no + 3)
            for t in range(KT):
                last = nc.tensor.transpose(sc[:, 0, t * P:(t + 1) * P], colmax[:, t * P:(t + 1) * P], ident[:, :])
            last.then_inc(sc_full, 1)

        def broadcast_rowmax(pe, m, slot_read=None):
            pe.wait_ge(sc_free, SP_FREES * (m + 1))
            if slot_read is not None:
                pe.wait_ge(*slot_read)
            for t in range(KT):
                last = nc.tensor.matmul(sc[:, 1, t * P:(t + 1) * P], rowmax[:, t:t + 1].to_broadcast([P, P]),
                                        ident[:, :], start=True, stop=True)
            last.then_inc(sc_full, 1)

        def weigh_values(pe, n, buf, pair, half):
            if pair == 0 and half == 0:
                pe.wait_ge(vh_ready, n + 1)
            pe.wait_ge(probs_ready, NCH * n + 4 * pair + 2 * half + 2 + START)
            for k in range(CK):
                for g in range(G):
                    qh, w2 = g // 2, g % 2
                    col = k * S + qh * HALF
                    probs = ring[:, 2 * half + w2, col:col + HALF]
                    if half == 1 and k == CK - 1 and g == G - 1:
                        pe.wait_ge(vexp_step, VSTEPS * (8 * n + pair + 1))
                        probs = vprobs[:, pair % 2, :]
                    last = nc.tensor.matmul(pv[g * VC:(g + 1) * VC, pair % 2, :], vh[:, buf, half * CK + k, :], probs,
                                            start=(half == 0 and k == 0), stop=(half == 1 and k == CK - 1))
            last.then_inc(slot_free, 2)

        def transpose_numer(pe, n, quad):
            pe.wait_ge(tr_read, 4 * n + quad + START)
            for pair in range(2):
                pe.wait_ge(pv_read, 8 * n + 2 * quad + pair + 1)
                for blk in range(4):
                    last = nc.tensor.transpose(tr[:, pair, blk * P:(blk + 1) * P],
                                               numer[:, pair, blk * P:(blk + 1) * P], ident[:, :])
            last.then_inc(tr_full, 1)

        def tile_attention(pe, i, n):
            pe.wait_ge(tile_in, 32 * (i + 1))
            pe.wait_ge(tr_read, 4 * n + 1 + START)
            nc.tensor.transpose(tr[:, 0, 0:P], tile_att[:, :], ident[:, :]).then_inc(tile_attT_ready, 1)

        def tile_projection(pe, i):
            pe.wait_ge(tile_attT_made, i + 1)
            nc.tensor.matmul(tr[:, 1, 0:E], tile_attT[:, :], wo_sb[:, :], start=True, stop=True).then_inc(tile_y, 1)

        def tile_transpose(pe, i):
            pe.wait_ge(tile_x1_made, i + 1 + START)
            nc.tensor.transpose(tr[:, 0, 0:P], tile_x1[:, :], ident[:, :]).then_inc(tile_x1T_ready, 1)

        def tile_router(pe, i):
            pe.wait_ge(tile_x1T_made, i + 1)
            nc.tensor.matmul(tr[:, 1, 0:NR], tile_x1T[:, :], rw_sb[:, :], start=True, stop=True).then_inc(tile_logits, 1)

        def tile_slice(pe, i, m, k):
            if k == 0:
                pe.wait_ge(tile_w1, 16 * (i + 1))
                pe.wait_ge(sc_free, SP_FREES * m + KT)
            elif k >= 2:
                pe.wait_ge(tile_hidden_copied, 4 * i + k - 1)
            for j in range(2 * FC):
                col = (2 * FC * k + j) * P
                last = nc.tensor.matmul(sc[:, k % 2, j * P:(j + 1) * P], tile_w[:, col:col + P], tile_x1T[:, :], start=True, stop=True)
            last.then_inc(tile_hidden, 1)

        def tile_part_two(pe, i, nxt, wi):
            if wi == 0:
                pe.wait_ge(tile_w2, 16 * (i + 1))
                pe.wait_ge(tile_gelu, i + 1)
                if nxt is not None:
                    pe.wait_ge(sc_free, SP_FREES * nxt + KT)
                else:
                    pe.wait_ge(diff_ready, KT * NH)
            for e in (2 * wi, 2 * wi + 1):
                for c in range(FC):
                    col = (e * FC + c) * P
                    last = nc.tensor.matmul(sc[:, 1, e * P:(e + 1) * P], tile_h[:, col:col + P], tile_w[:, col:col + P],
                                            start=(c == 0), stop=(c == FC - 1))
            if wi == 3:
                last.then_inc(tile_products, 1)

        def head_products(pe, n, nxt, tile_no=None, part=0):
            buf = 1 if part == 2 else 0
            for quad in range(4):
                for wi in range(4):
                    if quad == 2 and wi == 0 and part == 1 and tile_no is not None:
                        tile_router(pe, tile_no)
                    if wi == 0 and quad:
                        pe.wait_ge(pv_read, 8 * n + 2 * quad - 1)
                    weigh_values(pe, n, buf, 2 * quad + wi // 2, wi % 2)
                    if wi == 0 and quad:
                        if quad == 2 and part == 1 and tile_no is not None:
                            pe.wait_ge(tile_logits_made, tile_no + 1)
                        transpose_numer(pe, n, quad - 1)
                    if nxt is not None:
                        if quad < 2:
                            score_tile(pe, nxt, 4 * quad + wi)
                        elif quad == 3 and wi == 0:
                            transpose_colmax(pe, nxt, tile_no if part == 1 else None)
                        elif quad == 3 and wi == 1:
                            broadcast_rowmax(pe, nxt, [None, (tile_hidden_copied, 4 * tile_no + 4), (tile_added, tile_no + 1)][part]
                                             if tile_no is not None else None)
                    if tile_no is not None and part == 1:
                        if quad == 1 and wi:
                            if wi == 1:
                                tile_attention(pe, tile_no, n)
                            elif wi == 2:
                                tile_projection(pe, tile_no)
                            else:
                                tile_transpose(pe, tile_no)
                        elif quad == 2:
                            tile_slice(pe, tile_no, nxt, wi)
                    if tile_no is not None and part == 2 and quad == 2:
                        tile_part_two(pe, tile_no, nxt, wi)
            transpose_numer(pe, n, 3)

        def tensor_main(pe):
            pe.wait_ge(qk_loaded, 32)
            for k in range(KT):
                score_tile(pe, 0, k, first=True)
            transpose_colmax(pe, 0)
            broadcast_rowmax(pe, 0)
            with pe.Fori(0, FIRST_PAIR) as i:
                head_products(pe, 2 * i, 2 * i + 1, part=1)
                head_products(pe, 2 * i + 1, 2 * i + 2, part=2)
            with pe.Fori(0, PAIRS - FIRST_PAIR - 1) as i:
                n = 2 * (i + FIRST_PAIR)
                head_products(pe, n, n + 1, i, 1)
                head_products(pe, n + 1, n + 2, i, 2)
            head_products(pe, NH - 2, NH - 1, PAIRS - FIRST_PAIR - 1, 1)
            head_products(pe, NH - 1, None, PAIRS - FIRST_PAIR - 1, 2)

        def mask_keys(dve, m, first=False):
            if not first:
                dve.wait_ge(sc_full, SP_FULLS * m - 1)
            dve.wait_ge(qk_loaded, 32 * (m // H + 1) if not first else 32)
            nc.vector.tensor_scalar(km[:, :], kt_[:, :], headmask[:, bass.ds(m % H, 1)], None, ALU.mult).then_inc(km_ready, 1)

        def copy_scores(dve, m, k):
            dve.wait_ge(sc_full, SP_FULLS * m + k + 1)
            nc.vector.tensor_copy(scores[:, bass.ds(m % 2, 1), k, :].rearrange("p o s -> p (o s)"), sc[:, k % 2, :]).then_inc(sc_free, 1)

        def column_max(dve, m, r):
            dve.wait_ge(sc_free, SP_FREES * m + KT)
            apart(dve)
            last = nc.vector.tensor_reduce(colmax[:, r * QG:(r + 1) * QG],
                                           scores[:, bass.ds(m % 2, 1), :, r * QG:(r + 1) * QG].rearrange("p o k q -> p (o q) k"),
                                           axis=AX.X, op=ALU.max)
            if r == G - 1:
                last.then_inc(colmax_ready, 1)

        def row_max(dve, m):
            dve.wait_ge(sc_full, SP_FULLS * m + KT + 1)
            nc.vector.tensor_reduce(rowmax[:, :], sc[:, 0, :].rearrange("p (t k) -> p t k", k=P), axis=AX.X,
                                    op=ALU.max).then_inc(sc_free, 1)

        def subtract_max(dve, m, k):
            if k == 0:
                dve.wait_ge(sc_full, SP_FULLS * (m + 1))
            tile_ = scores[:, bass.ds(m % 2, 1), k, :].rearrange("p o s -> p (o s)")
            nc.vector.tensor_tensor(tile_, tile_, sc[:, 1, :], ALU.subtract).then_inc(diff_ready, 1)

        def exponentials(dve, m, pair, first=False):
            base = VSTEPS * (8 * m + pair)
            y = scores[:, bass.ds(m % 2, 1), KT - 1, HALF:S].rearrange("p o s -> p (o s)")
            rest, power, probs = vrest[:, :], vpower[:, :], vprobs[:, pair % 2, :]
            then = stepper(dve, vexp_step, base, [0])
            dve.wait_ge(diff_ready, KT * (m + 1))
            if not first:
                dve.wait_ge(vexp_step, base)
            apart(dve)
            then(nc.vector.tensor_scalar(rest, y, scales_log2[:, bass.ds((2 * pair + 1) * H + m % H, 1)], EXP2_LOW, ALU.mult, ALU.max))
            then(nc.vector.tensor_scalar(power, rest, MAGIC, None, ALU.add))
            then(nc.vector.scalar_tensor_tensor(rest, power, -MAGIC, rest, ALU.add, ALU.subtract))
            then(nc.vector.tensor_scalar(power.bitcast(I32), power, -(MAGIC - 127.0), 2.0 ** 23, ALU.add, ALU.mult))
            then(nc.vector.tensor_scalar(probs, rest, -EXP2[4], EXP2[3], ALU.mult, ALU.add))
            then(nc.vector.tensor_tensor(probs, probs, rest, ALU.mult))
            for coefficient in (-EXP2[2], EXP2[1], -EXP2[0]):
                then(nc.vector.scalar_tensor_tensor(probs, probs, coefficient, rest, ALU.add, ALU.mult))
            nc.vector.scalar_tensor_tensor(probs, probs, 1.0, power, ALU.add, ALU.mult).then_inc(vexp_step, 1)

        def copy_numer(dve, n, quad, pair):
            dve.wait_ge(slot_free, SLOTS + NCH * n + 8 * quad + 4 * (pair + 1))
            dve.wait_ge(tr_full, 4 * n + quad + START)
            nc.vector.tensor_copy(numer[:, pair, :], pv[:, pair, :]).then_inc(pv_read, 1)

        def normalise(dve, n, quad):
            dve.wait_ge(tr_full, 4 * n + quad + 1 + START)
            blocks = tr[:, :, :].rearrange("p a (m c) -> p (a m) c", c=VC)
            nc.vector.reciprocal(recip[:, :], blocks[:, :, D]).then_inc(norm_step, 1)
            dve.wait_ge(norm_step, 8 * n + 2 * quad + 1)
            nc.vector.tensor_tensor(coef[:, :], recip[:, :],
                                    wl_wide[:, 2 * quad:2 * quad + 2, :, :].rearrange("p a t w -> p (a t w)"),
                                    ALU.mult).then_inc(norm_step, 1)
            dve.wait_ge(norm_step, 8 * n + 2 * quad + 2)
            nc.vector.tensor_tensor(parts[:, 2 * quad:2 * quad + 2, :, :, :].rearrange("p a t w d -> p (a t w) d"), blocks[:, :, 0:D],
                                    coef[:, :].rearrange("p (g o) -> p g o", o=1).to_broadcast([P, 32, D]),
                                    ALU.mult).then_inc(tr_read, 1)

        def sum_wavelengths(dve, n):
            dve.wait_ge(tr_read, 4 * (n + 1) + START)
            dve.wait_ge(att_stored, 32 * (n // H) + START)
            nc.vector.tensor_reduce(att[:, :, bass.ds((n % H) * D, D)], parts[:, :, :, :, :].rearrange("p a t w d -> p t d a w"),
                                    axis=AX.XY, op=ALU.add).then_inc(att_made, 1)

        def tile_part_one_vector(dve, i, step, then):
            if step == 0:
                dve.wait_ge(tile_in, 32 * (i + 1))
                dve.wait_ge(tile_attT_ready, i + 1)
                nc.vector.tensor_copy(tile_attT[:, :], tr[:, 0, 0:P]).then_inc(tile_attT_made, 1)
                then(nc.vector.tensor_tensor(tile_z[:, :], tile_x[:, :], bo_sb[:, :], ALU.add))
            elif step == 1:
                dve.wait_ge(tile_y, i + 1)
                then(nc.vector.tensor_tensor(tile_z[:, :], tile_z[:, :], tr[:, 1, 0:E], ALU.add))
                layer_norm(then, tile_z[:, :], tile_x1[:, :], 1, t_norm, dve).then_inc(tile_x1_made, 1)
            elif step == 2:
                dve.wait_ge(tile_x1T_ready, i + 1)
                nc.vector.tensor_copy(tile_x1T[:, :], tr[:, 0, 0:P]).then_inc(tile_x1T_made, 1)
            elif step == 3:
                dve.wait_ge(tile_logits, i + 1)
                then(nc.vector.tensor_tensor(t_lg, tr[:, 1, 0:NR].rearrange("p (t r) -> p t r", r=NR), over_tiles(rb_sb, 1), ALU.add))
                then(nc.vector.tensor_reduce(t_four[0], t_lg, axis=AX.X, op=ALU.max))
                nc.vector.tensor_tensor(t_lg, t_lg, wide(t_four[0], 1), ALU.subtract).then_inc(tile_logits_made, 1)

        def copy_hidden(dve, i, k):
            dve.wait_ge(tile_hidden, 4 * i + k + 1)
            if k == 0:
                dve.wait_ge(tile_products, i + START)
            nc.vector.tensor_copy(tile_h[:, k * S:(k + 1) * S], sc[:, k % 2, :]).then_inc(tile_hidden_copied, 1)

        def tile_gates(dve, i, then):
            dve.wait_ge(tile_exp, i + 1)
            route(then, t_route, t_four, 1)
            then(nc.vector.scalar_tensor_tensor(tile_z[:, :], tile_x1[:, :], t_route[6][:, 0, NE:NE + 1], tile_x1[:, :], ALU.mult, ALU.add))

        def tile_finish(dve, i, then):
            dve.wait_ge(tile_products, i + 1 + START)
            for e in range(NE - 1):
                then(nc.vector.scalar_tensor_tensor(tile_z[:, :], sc[:, 1, e * P:(e + 1) * P], t_route[6][:, 0, e:e + 1],
                                                    tile_z[:, :], ALU.mult, ALU.add))
            e = NE - 1
            nc.vector.scalar_tensor_tensor(tile_z[:, :], sc[:, 1, e * P:(e + 1) * P], t_route[6][:, 0, e:e + 1],
                                           tile_z[:, :], ALU.mult, ALU.add).then_inc(tile_added, 1)
            dve.wait_ge(tile_added, i + 1)
            dve.wait_ge(tile_out_free, i + START)
            layer_norm(then, tile_z[:, :], tile_out[:, :], 1, t_norm, dve).then_inc(tile_done, 1)

        def vector_head(dve, n, nxt, i=None, part=0, then=None, keys_for=None):
            shares = {0: 1, 1: 2, 3: 3, 5: 4, 8 if part == 1 else 7: 5, 9: 6, 13 if part else 11: 7}
            if nxt is not None:
                dve.wait_ge(probs_ready, NCH * n + START)
            for quad in range(4):
                for wi in range(4):
                    if quad == 2 and wi == 0 and part == 1:
                        tile_part_one_vector(dve, i, 3, then)
                    if wi == 0 and quad:
                        normalise(dve, n, quad - 1)
                    if wi % 2 == 1:
                        copy_numer(dve, n, quad, wi // 2)
                    if nxt is not None:
                        if quad < 2:
                            copy_scores(dve, nxt, 4 * quad + wi)
                        elif quad == 2:
                            column_max(dve, nxt, wi)
                        elif wi == 0:
                            row_max(dve, nxt)
                        elif wi < 3:
                            for k in range(4 * (wi - 1), 4 * wi):
                                subtract_max(dve, nxt, k)
                            if wi == 2 and keys_for is not None:
                                mask_keys(dve, keys_for)
                    if quad == 1 and wi and part == 1:
                        tile_part_one_vector(dve, i, wi - 1, then)
                    if quad == 2 and part == 1:
                        copy_hidden(dve, i, wi)
                    if quad == 2 and wi == 3 and part == 2:
                        tile_finish(dve, i, then)
                    if quad == 1 and wi == 2 and part == 2:
                        tile_gates(dve, i, then)
                    at = 4 * quad + wi
                    if at in shares:
                        exponentials(dve, n, shares[at])
                    elif nxt is not None and at == 15:
                        exponentials(dve, nxt, 0)
            normalise(dve, n, 3)
            sum_wavelengths(dve, n)

        def vector_main(dve):
            mask_keys(dve, 0, first=True)
            for k in range(KT):
                copy_scores(dve, 0, k)
            for r in range(G):
                column_max(dve, 0, r)
            row_max(dve, 0)
            for k in range(KT):
                subtract_max(dve, 0, k)
            mask_keys(dve, 1)
            exponentials(dve, 0, 0, first=True)
            with dve.Fori(0, H) as n:
                vector_head(dve, n, n + 1, keys_for=n + 2)

            def pair(i, last):
                n = 2 * (i + FIRST_PAIR)
                counted = [0]
                then = stepper(dve, tile_step, TILE_STEPS * i, counted)
                vector_head(dve, n, n + 1, i, 1, then, keys_for=None if last else n + 2)
                vector_head(dve, n + 1, None if last else n + 2, i, 2, then, keys_for=None if last else n + 3)
                assert counted[0] == TILE_STEPS, counted
            with dve.Fori(0, PAIRS - FIRST_PAIR - 1) as i:
                pair(i, False)
            pair(PAIRS - FIRST_PAIR - 1, True)
        TILE_STEPS = 60

        gen_masked, gen_scores, gen_read = sem("gen_masked"), sem("gen_scores"), sem("gen_read")
        gen_step = sem("gen_step")
        gen_sine, gen_exp = sem("gen_sine"), sem("gen_exp")
        gen_angle, gen_shifted = sem("gen_angle"), sem("gen_shifted")
        gen_weighed = sem("gen_weighed")
        gen_tr, gen_tr_read, gen_pv = sem("gen_tr"), sem("gen_tr_read"), sem("gen_pv")
        g_raw, g_s, g_x, g_n, g_t, g_c = (scores[:, 0, i, :] for i in range(6))
        g_acc = scores[:, 0, 6, :]
        g_pT = scores[:, 0, 7, :]
        g_p = scores[:, 1, 0, :]
        g_max, g_neg, g_z, g_coef = (rowmax[:, i:i + 1] for i in range(4))
        GEN_STEPS = 11

        def sync_general(sp):
            with sp.Fori(0, B) as b:
                sp.wait_ge(att_made, H * KT * b + START)
                load_qk(sp, b)
                load_v(sp, b)
                sp.wait_ge(att_made, H * KT * (b + 1) + START)
                store_att(sp, b)

        def tensor_general(pe):
            with pe.Fori(0, NH) as n:
                with pe.Fori(0, KT) as t:
                    j = n * KT + t
                    pe.wait_ge(gen_masked, j + 1)
                    for half in range(2):
                        cols = slice(half * HALF, (half + 1) * HALF)
                        last = nc.tensor.matmul(sc[:, 0, cols], km[:, 0:P], kt_[:, cols], start=True, stop=True)
                    last.then_inc(gen_scores, 1)
                    pe.wait_ge(gen_weighed, 2 * W * (j + 1))
                    for k in range(KT):
                        last = nc.tensor.transpose(sc[:, 1, k * P:(k + 1) * P], g_acc[:, k * P:(k + 1) * P], ident[:, :])
                    last.then_inc(gen_tr, 1)
                    pe.wait_ge(gen_tr_read, j + 1)
                    for k in range(KT):
                        last = nc.tensor.matmul(pv[:, 0, 0:D], g_pT[:, k * P:(k + 1) * P],
                                                vv[:, k, bass.ds((n % H) * D, D)], start=(k == 0), stop=(k == KT - 1))
                    last.then_inc(gen_pv, 1)

        def scalar_general(act):
            with act.Fori(0, NH * KT) as j:
                with act.Fori(0, W) as w:
                    act.wait_ge(gen_angle, j * W + w + 1)
                    nc.scalar.activation(g_c, g_t, ACT.Sin, scale=0.5).then_inc(gen_sine, 1)
                    act.wait_ge(gen_shifted, j * W + w + 1)
                    nc.scalar.activation(g_p, g_t, ACT.Exp, bias=g_neg, accum_out=g_z).then_inc(gen_exp, 1)

        def vector_general(dve):
            with dve.Fori(0, NH) as n:
                with dve.Fori(0, KT) as t:
                    j = n * KT + t
                    dve.wait_ge(qk_loaded, 32 * (n // H + 1))
                    dve.wait_ge(v_loaded, 16 * (n // H + 1))
                    dve.wait_ge(gen_scores, j + START)
                    nc.vector.tensor_scalar(km[:, 0:P], qt[:, bass.ds(t * P, P)], headmask[:, bass.ds(n % H, 1)], None,
                                            ALU.mult).then_inc(gen_masked, 1)
                    dve.wait_ge(gen_scores, j + 1 + START)
                    nc.vector.tensor_copy(g_raw, sc[:, 0, :])
                    dve.wait_ge(gen_tr, j + START)
                    nc.vector.memset(g_acc, 0.0).then_inc(gen_read, 1)
                    with dve.Fori(0, W) as w:
                        dve.wait_ge(gen_read, j + 1)
                        i = j * W + w
                        done = i * GEN_STEPS

                        nc.vector.tensor_scalar(g_s, g_raw, scales[:, bass.ds(w * H + n % H, 1)], None, ALU.mult).then_inc(gen_step, 1)
                        dve.wait_ge(gen_step, done + 1)
                        nc.vector.scalar_tensor_tensor(g_x, g_s, KERR, g_s, ALU.mult, ALU.mult).then_inc(gen_step, 1)
                        dve.wait_ge(gen_step, done + 2)
                        nc.vector.tensor_scalar(g_n, g_x, 1.0 / (2.0 * np.pi), MAGIC, ALU.mult, ALU.add).then_inc(gen_step, 1)
                        dve.wait_ge(gen_step, done + 3)
                        nc.vector.tensor_scalar(g_n, g_n, MAGIC, None, ALU.subtract).then_inc(gen_step, 1)
                        src = g_x
                        for part_no, part in enumerate(TWO_PI):
                            dve.wait_ge(gen_step, done + 4 + part_no)
                            nc.vector.scalar_tensor_tensor(g_t, g_n, -part, src, ALU.mult, ALU.add).then_inc(gen_step, 1)
                            src = g_t
                        dve.wait_ge(gen_step, done + 7)
                        nc.vector.tensor_scalar(g_t, g_t, PI, -PI, ALU.min, ALU.max).then_inc(gen_angle, 1)
                        dve.wait_ge(gen_sine, i + 1)
                        nc.vector.tensor_tensor(g_x, g_c, g_c, ALU.mult).then_inc(gen_step, 1)
                        dve.wait_ge(gen_step, done + 8)
                        nc.vector.tensor_scalar(g_x, g_x, -2.0, 1.0, ALU.mult, ALU.add).then_inc(gen_step, 1)
                        dve.wait_ge(gen_step, done + 9)
                        nc.vector.tensor_tensor(g_t, g_s, g_x, ALU.mult).then_inc(gen_step, 1)
                        dve.wait_ge(gen_step, done + 10)
                        nc.vector.tensor_reduce(g_neg, g_t, axis=AX.X, op=ALU.max, negate=True).then_inc(gen_shifted, 1)
                        dve.wait_ge(gen_exp, i + 1)
                        nc.vector.reciprocal(g_max, g_z).then_inc(gen_step, 1)
                        dve.wait_ge(gen_step, done + 11)
                        nc.vector.tensor_tensor(g_coef, g_max, wl_weight[:, bass.ds(w, 1)], ALU.mult).then_inc(gen_weighed, 1)
                        dve.wait_ge(gen_weighed, 2 * i + 1)
                        nc.vector.scalar_tensor_tensor(g_acc, g_p, g_coef, g_acc, ALU.mult, ALU.add).then_inc(gen_weighed, 1)
                        dve.wait_ge(gen_weighed, 2 * i + 2)
                        apart(dve)
                    dve.wait_ge(gen_tr, j + 1 + START)
                    nc.vector.tensor_copy(g_pT, sc[:, 1, :]).then_inc(gen_tr_read, 1)
                    dve.wait_ge(gen_pv, j + 1)
                    dve.wait_ge(att_stored, 32 * (n // H) + START)
                    nc.vector.tensor_copy(att[:, bass.ds((t % 4) * 2 + t // 4, 1), bass.ds((n % H) * D, D)].rearrange("p o d -> p (o d)"),
                                          pv[:, 0, 0:D]).then_inc(att_made, 1)

        weights = ring[:, :, :].rearrange("p s c -> p (s c)")
        w1_sb = weights[:, 0:NE * F].rearrange("p (e f) -> p e f", f=F)
        w2_sb = weights[:, NE * F:2 * NE * F].rearrange("p (e c d) -> p e c d", e=NE, d=E)
        pool_area = scores[:, :, :, :].rearrange("p a k s -> p (a k s)")

        def area(i, n=1):
            return pool_area[:, i * HALF:(i + n) * HALF]
        tiles = lambda a: a.rearrange("p (t e) -> p t e", e=E)
        xg, ag, aT, z, x1, x1T, z2, yo = (area(i) for i in range(8))
        hT = area(8, 2 * FC).rearrange("p (a c t) -> p a c t", a=2, t=HALF)
        g_norm = norm_views(area(16), GT)
        g_route = route_views(area(17), GT)
        lg, ex, gates = g_route[0], g_route[1], g_route[6]
        g_four = [area(18)[:, i * GT:(i + 1) * GT] for i in range(3)]

        ff_weights = sem("ff_weights")
        ff_in = sem("ff_in")
        ff_attT, ff_attT_made = sem("ff_attT"), sem("ff_attT_made")
        ff_y, ff_x1, ff_x1T, ff_x1T_made = sem("ff_y"), sem("ff_x1"), sem("ff_x1T"), sem("ff_x1T_made")
        ff_logits, ff_logits_made, ff_exp = sem("ff_logits"), sem("ff_logits_made"), sem("ff_exp")
        ff_hidden, ff_gelu = sem("ff_hidden"), sem("ff_gelu")
        ff_expert, ff_added = sem("ff_expert"), sem("ff_added")
        ff_step = sem("ff_step")
        ff_out, ff_stored = sem("ff_out"), sem("ff_stored")

        def sync_ff(sp, groups):
            first = NG - groups

            def load(g):
                sp.dma_start(tiles(xg), x_tiles[bass.ds((g + first) * GT, GT)].rearrange("t p e -> p t e")).then_inc(ff_in, 16)
                sp.dma_start(tiles(ag), att_dram[bass.ds((g + first) * GT, GT)].rearrange("t p e -> p t e")).then_inc(ff_in, 16)

            def store(g):
                sp.dma_start(out_tiles[bass.ds((g + first) * GT, GT)].rearrange("t p e -> p t e"), tiles(yo)).then_inc(ff_stored, 16)

            sp.wait_ge(att_stored, 32 * B + START)
            load(0)
            sp.dma_start(w1_sb.rearrange("p e f -> p (e f)"), w1.rearrange("d e f -> d (e f)")).then_inc(ff_weights, 16)
            sp.dma_start(w2_sb.rearrange("p e c d -> p (e c d)"), w2.rearrange("p e c d -> p (e c d)")).then_inc(ff_weights, 16)
            with sp.Fori(1, groups) as g:
                sp.wait_ge(ff_x1, g + START)
                load(g)
                sp.wait_ge(ff_out, g)
                store(g - 1)
            sp.wait_ge(ff_out, groups)
            store(groups - 1)
            sp.wait_ge(ff_stored, 16 * groups + START)

        def hidden(pe, g, e):
            for c in range(FC):
                i = e * FC + c
                if i < 4:
                    pe.wait_ge(ff_gelu, NE * FC * g + START)
                else:
                    pe.wait_ge(ff_gelu, NE * FC * g + i - 3 + START)
                nc.tensor.matmul(sc[:, (i // 2) % 2, (i % 2) * HALF:(i % 2 + 1) * HALF], w1_sb[:, e, c * P:(c + 1) * P], x1T,
                                 start=True, stop=True).then_inc(ff_hidden, 1)

        def expert_out(pe, g, e):
            pe.wait_ge(ff_gelu, NE * FC * g + (e + 1) * FC + START)
            pe.wait_ge(ff_added, (NE * g + e - 1 if e >= 1 else NE * g) + START)
            for t in range(GT):
                for c in range(FC):
                    last = nc.tensor.matmul(tr[:, e % 2, t * P:(t + 1) * P], hT[:, e % 2, c, t * P:(t + 1) * P], w2_sb[:, e, c, :],
                                            start=(c == 0), stop=(c == FC - 1))
            last.then_inc(ff_expert, 1)

        def tensor_ff(pe, groups):
            with pe.Fori(0, groups) as g:
                pe.wait_ge(ff_in, 32 * (g + 1))
                for t in range(GT):
                    last = nc.tensor.transpose(pv[:, 0, t * P:(t + 1) * P], tiles(ag)[:, t, :], ident[:, :])
                last.then_inc(ff_attT, 1)
                pe.wait_ge(ff_attT_made, g + 1)
                for t in range(GT):
                    last = nc.tensor.matmul(pv[:, 1, t * P:(t + 1) * P], aT[:, t * P:(t + 1) * P], wo_sb[:, :], start=True, stop=True)
                last.then_inc(ff_y, 1)
                pe.wait_ge(ff_x1, g + 1 + START)
                for t in range(GT):
                    last = nc.tensor.transpose(pv[:, 0, t * P:(t + 1) * P], tiles(x1)[:, t, :], ident[:, :])
                last.then_inc(ff_x1T, 1)
                pe.wait_ge(ff_x1T_made, g + 1)
                for t in range(GT):
                    last = nc.tensor.matmul(pv[:, 1, t * NR:(t + 1) * NR], x1T[:, t * P:(t + 1) * P], rw_sb[:, :], start=True, stop=True)
                last.then_inc(ff_logits, 1)
                pe.wait_ge(ff_weights, 32)
                hidden(pe, g, 0)
                for e in range(NE):
                    if e + 1 < NE:
                        hidden(pe, g, e + 1)
                    expert_out(pe, g, e)

        def scalar_ff(act, groups):
            with act.Fori(0, groups) as g:
                act.wait_ge(ff_logits_made, g + 1)
                nc.scalar.activation(ex, lg, ACT.Exp).then_inc(ff_exp, 1)
                for i in range(NE * FC):
                    act.wait_ge(ff_hidden, NE * FC * g + i + 1)
                    if i // FC >= 2 and i % FC == 0:
                        act.wait_ge(ff_expert, NE * g + i // FC - 1 + START)
                    elif i % FC == 0:
                        act.wait_ge(ff_expert, NE * g + START)
                    nc.scalar.activation(hT[:, (i // FC) % 2, i % FC, :], sc[:, (i // 2) % 2, (i % 2) * HALF:(i % 2 + 1) * HALF],
                                         ACT.Gelu).then_inc(ff_gelu, 1)

        def vector_ff(dve, groups):
            def body(g, then):
                dve.wait_ge(ff_in, 32 * (g + 1))
                then(nc.vector.tensor_tensor(tiles(z), tiles(xg), over_tiles(bo_sb, GT), ALU.add))
                dve.wait_ge(ff_attT, g + 1)
                nc.vector.tensor_copy(aT, pv[:, 0, :]).then_inc(ff_attT_made, 1)
                dve.wait_ge(ff_y, g + 1)
                then(nc.vector.tensor_tensor(z, z, pv[:, 1, :], ALU.add))
                layer_norm(then, z, x1, GT, g_norm, dve).then_inc(ff_x1, 1)
                dve.wait_ge(ff_x1T, g + 1)
                nc.vector.tensor_copy(x1T, pv[:, 0, :]).then_inc(ff_x1T_made, 1)
                dve.wait_ge(ff_logits, g + 1)
                then(nc.vector.tensor_tensor(lg, pv[:, 1, 0:GT * NR].rearrange("p (t r) -> p t r", r=NR), over_tiles(rb_sb, GT), ALU.add))
                then(nc.vector.tensor_reduce(g_four[0], lg, axis=AX.X, op=ALU.max))
                nc.vector.tensor_tensor(lg, lg, wide(g_four[0], GT), ALU.subtract).then_inc(ff_logits_made, 1)
                dve.wait_ge(ff_exp, g + 1)
                route(then, g_route, g_four, GT)
                for t in range(GT):
                    last = nc.vector.scalar_tensor_tensor(tiles(z2)[:, t, :], tiles(x1)[:, t, :], gates[:, t, NE:NE + 1],
                                                          tiles(x1)[:, t, :], ALU.mult, ALU.add)
                then(last)
                for e in range(NE):
                    dve.wait_ge(ff_expert, NE * g + e + 1 + START)
                    if e:
                        dve.wait_ge(ff_added, NE * g + e + START)
                    for t in range(GT):
                        last = nc.vector.scalar_tensor_tensor(tiles(z2)[:, t, :], tr[:, e % 2, t * P:(t + 1) * P], gates[:, t, e:e + 1],
                                                              tiles(z2)[:, t, :], ALU.mult, ALU.add)
                    last.then_inc(ff_added, 1)
                dve.wait_ge(ff_added, NE * (g + 1) + START)
                dve.wait_ge(ff_stored, 16 * g + START)
                layer_norm(then, z2, yo, GT, g_norm, dve).then_inc(ff_out, 1)

            with dve.Fori(0, groups) as g:
                counted = [0]
                body(g, stepper(dve, ff_step, FF_STEPS * g, counted))
                assert counted[0] == FF_STEPS, counted
        FF_STEPS = 53

        @block.sync
        def _(sp):
            sync_setup(sp)
            sp.wait_ge(qkv_stored, 48 * B + START)
            sp.wait_ge(flag_ready, 1)
            safe = sp.value_load(flag[0:1, 0:1], min_val=0, max_val=1)
            with sp.If(safe == 1):
                sync_main(sp)
                sync_ff(sp, TAIL)
            with sp.Else():
                sync_general(sp)
                sync_ff(sp, NG)

        @block.gpsimd
        def _(pool):
            pool_setup(pool)
            pool.wait_ge(flag_ready, 1)
            safe = pool.value_load(flag[0:1, 0:1], min_val=0, max_val=1)
            with pool.If(safe == 1):
                pool_main(pool)
            with pool.Else():
                pool.nop()

        @block.scalar
        def _(act):
            scalar_setup(act)
            act.wait_ge(flag_ready, 1)
            safe = act.value_load(flag[0:1, 0:1], min_val=0, max_val=1)
            with act.If(safe == 1):
                scalar_main(act)
                scalar_ff(act, TAIL)
            with act.Else():
                scalar_general(act)
                scalar_ff(act, NG)

        @block.tensor
        def _(pe):
            tensor_setup(pe)
            pe.wait_ge(flag_ready, 1)
            safe = pe.value_load(flag[0:1, 0:1], min_val=0, max_val=1)
            with pe.If(safe == 1):
                tensor_main(pe)
                tensor_ff(pe, TAIL)
            with pe.Else():
                tensor_general(pe)
                tensor_ff(pe, NG)

        @block.vector
        def _(dve):
            vector_setup(dve)
            dve.wait_ge(flag_ready, 1)
            safe = dve.value_load(flag[0:1, 0:1], min_val=0, max_val=1)
            with dve.If(safe == 1):
                vector_main(dve)
                vector_ff(dve, TAIL)
            with dve.Else():
                vector_general(dve)
                vector_ff(dve, NG)


_INS = ["L0_attn_x", "L0_attn_Wq", "L0_attn_bq", "L0_attn_Wk", "L0_attn_bk", "L0_attn_Wv", "L0_attn_bv",
        "L0_attn_Wo", "L0_attn_bo", "L0_attn_phase_modulators", "L0_attn_interference_weights",
        "L0_ffn_router_w", "L0_ffn_router_b", "L0_ffn_w1", "L0_ffn_w2"]


def lay_out(name, a):
    a = np.asarray(a)
    if name == "L0_ffn_w1":
        a = a.transpose(1, 0, 2)
    elif name == "L0_ffn_w2":
        a = a.reshape(NE, FC, P, E).transpose(2, 0, 1, 3)
    return np.ascontiguousarray(a)


def kernel(**inputs):
    import concourse.bacc as bacc
    from concourse.bass_utils import run_bass_kernel_spmd

    nc = bacc.Bacc("TRN2", target_bir_lowering=False, num_devices=1)
    arrays, args = {}, []
    for name in _INS:
        a = lay_out(name, inputs[name])
        arrays[f"in_{name}"] = a
        args.append(nc.dram_tensor(f"in_{name}", a.shape, mybir.dt.from_np(a.dtype), kind="ExternalInput").ap())
    args.append(nc.dram_tensor("out", (B, S, E), FP32, kind="ExternalOutput").ap())
    build(nc, *args)
    r = run_bass_kernel_spmd(nc, [arrays], core_ids=[0])
    return r.results[0]["out"]
```
